# Optimizing a Trainium2 kernel written in Bass

```python
import numpy as np
import jax
import jax.numpy as jnp

def _softmax(x, axis=-1):
    return jax.nn.softmax(x, axis=axis)

def _gelu(x):
    return jax.nn.gelu(x, approximate=True)

def _silu(x):
    return jax.nn.silu(x)

def _sigmoid(x):
    return jax.nn.sigmoid(x)

def _layernorm(x, axis=-1, eps=1e-05):
    m = jnp.mean(x, axis=axis, keepdims=True)
    v = jnp.var(x, axis=axis, keepdims=True)
    return (x - m) / jnp.sqrt(v + eps)

def _scatter_add(tgt, idx, src, axis=0):
    return tgt.at[idx].add(src)

def _segment_sum(src, seg, n):
    return jax.ops.segment_sum(src, seg, n)
kernel_name = 'mk_gnn_ffn_d1_gnn_r8_6a7884'

def setup_inputs(seed: int=0):
    np.random.seed(seed)
    _w = jnp.asarray

    def _rec_inputs():
        import jax
        import jax.numpy as jnp
        _gk = jax.random.key(seed)
        x = -0.0003713 + 1 * jax.random.normal(jax.random.fold_in(_gk, 1), (12500, 256), jnp.float32)
        src = jax.random.randint(jax.random.fold_in(_gk, 2), (200000,), 0, 12500, jnp.int32)
        dst = jnp.minimum((12500 * jax.random.uniform(jax.random.fold_in(_gk, 3), (200000,)) ** 2.0).astype(jnp.int32), 99999)
        _o = jnp.argsort(dst, stable=True)
        src = src[_o]
        dst = dst[_o]
        edge_attr_16 = 0.000398945 + 1.00003 * jax.random.normal(jax.random.fold_in(_gk, 11), (200000, 16), jnp.float32)
        return (x, src, dst, edge_attr_16)
    x, src, dst, edge_attr_16 = _rec_inputs()

    def _L0_gnn_setup():
        import jax, jax.numpy as jnp
        import numpy as np
        N, E = (6250, 50000)
        HEADS, DIMS, EDGE_DIM = (4, 64, 16)
        FEAT = HEADS * DIMS
        NEG_SLOPE = 0.2

        def _gatv2(x, edge_index, edge_attr, W_l, b_l, W_r, b_r, W_e, att, bias):
            n = x.shape[0]
            src, dst = (edge_index[0], edge_index[1])
            x_l = (x @ W_l.T + b_l).reshape(n, HEADS, DIMS)
            x_r = (x @ W_r.T + b_r).reshape(n, HEADS, DIMS)
            ones = jnp.ones((src.shape[0],), x.dtype)
            deg = jax.ops.segment_sum(ones, dst, num_segments=n)
            loop_attr = jax.ops.segment_sum(edge_attr, dst, num_segments=n)
            loop_attr = loop_attr / jnp.clip(deg, 1.0, None)[:, None]
            loop = jnp.arange(n, dtype=src.dtype)
            src = jnp.concatenate([src, loop])
            dst = jnp.concatenate([dst, loop])
            e_attr = jnp.concatenate([edge_attr, loop_attr], axis=0)
            e_feat = (e_attr @ W_e.T).reshape(-1, HEADS, DIMS)
            s = x_l[src] + x_r[dst] + e_feat
            s = jax.nn.leaky_relu(s, NEG_SLOPE)
            alpha = jnp.einsum('ehc,hc->eh', s, att)
            amax = jax.ops.segment_max(alpha, dst, num_segments=n)
            ex = jnp.exp(alpha - amax[dst])
            denom = jax.ops.segment_sum(ex, dst, num_segments=n)
            alpha = ex / (denom[dst] + 1e-16)
            out = jax.ops.segment_sum(alpha[..., None] * x_l[src], dst, num_segments=n)
            return out.reshape(n, FEAT) + bias
        key = jax.random.key(seed)
        ks = jax.random.split(key, 10)
        s = 0.05
        return {'x': jax.random.normal(ks[0], (N, FEAT), jnp.float32), 'edge_index': jax.random.randint(ks[1], (2, E), 0, N, jnp.int64), 'edge_attr': jax.random.normal(ks[2], (E, EDGE_DIM), jnp.float32), 'W_l': jax.random.normal(ks[3], (FEAT, FEAT), jnp.float32) * s, 'b_l': jnp.zeros((FEAT,), jnp.float32), 'W_r': jax.random.normal(ks[4], (FEAT, FEAT), jnp.float32) * s, 'b_r': jnp.zeros((FEAT,), jnp.float32), 'W_e': jax.random.normal(ks[5], (FEAT, EDGE_DIM), jnp.float32) * s, 'att': jax.random.normal(ks[6], (HEADS, DIMS), jnp.float32) * s, 'bias': jnp.zeros((FEAT,), jnp.float32)}
    _L0_gnn_all = _L0_gnn_setup()
    _L0_gnn_in = {k: v for k, v in _L0_gnn_all.items() if k in ('W_l', 'b_l', 'W_r', 'b_r', 'W_e', 'att', 'bias')}
    del _L0_gnn_all

    def _L0_ffn_setup():
        import jax, jax.numpy as jnp
        import numpy as np
        B, N, D = (16, 512, 256)
        NUM_EXPERTS, TOP_K, HEADS = (4, 2, 4)
        N_EDGES = 131072
        LN_EPS = 1e-05

        def _layernorm(x, g, b):
            mu = x.mean(-1, keepdims=True)
            var = ((x - mu) ** 2).mean(-1, keepdims=True)
            return (x - mu) * jax.lax.rsqrt(var + LN_EPS) * g + b

        def _forward(x, edge_index, W_gat, att_src, att_dst, b_gat, ln_gamma, ln_beta, W1, b1, W2, b2):
            Bc, Nc, Dc = x.shape
            M = Bc * Nc
            x_flat = x.reshape(M, Dc)
            h = (x_flat @ W_gat).reshape(M, HEADS, NUM_EXPERTS)
            loops = jnp.arange(M, dtype=edge_index.dtype)
            src = jnp.concatenate([edge_index[0], loops])
            dst = jnp.concatenate([edge_index[1], loops])
            a_src = (h * att_src).sum(-1)
            a_dst = (h * att_dst).sum(-1)
            e = jax.nn.leaky_relu(a_src[src] + a_dst[dst], negative_slope=0.2)
            e_max = jax.ops.segment_max(e, dst, num_segments=M)
            ee = jnp.exp(e - e_max[dst])
            denom = jax.ops.segment_sum(ee, dst, num_segments=M)
            alpha = ee / (denom[dst] + 1e-16)
            msg = h[src] * alpha[:, :, None]
            agg = jax.ops.segment_sum(msg, dst, num_segments=M).reshape(M, HEADS * NUM_EXPERTS) + b_gat
            scores = _layernorm(agg, ln_gamma, ln_beta).reshape(M, HEADS, NUM_EXPERTS).mean(1)
            scores = scores.reshape(Bc, Nc, NUM_EXPERTS)
            topk_s, topk_i = jax.lax.top_k(scores, TOP_K)
            w = jax.nn.softmax(topk_s, axis=-1)
            out = jnp.zeros_like(x)
            for ei in range(NUM_EXPERTS):
                g = jnp.where(topk_i == ei, w, 0.0).sum(-1)
                hh = jax.nn.gelu(x @ W1[ei] + b1[ei], approximate=False)
                out = out + g[..., None] * (hh @ W2[ei] + b2[ei])
            return out
        key = jax.random.key(seed)
        ks = jax.random.split(key, 8)
        s = 0.05
        return {'x': jax.random.normal(ks[0], (B, N, D), jnp.float32), 'W_gat': jax.random.normal(ks[1], (D, HEADS * NUM_EXPERTS), jnp.float32) * s, 'att_src': jax.random.normal(ks[2], (HEADS, NUM_EXPERTS), jnp.float32) * s, 'att_dst': jax.random.normal(ks[3], (HEADS, NUM_EXPERTS), jnp.float32) * s, 'b_gat': jnp.zeros((HEADS * NUM_EXPERTS,), jnp.float32), 'ln_gamma': jnp.ones((HEADS * NUM_EXPERTS,), jnp.float32), 'ln_beta': jnp.zeros((HEADS * NUM_EXPERTS,), jnp.float32), 'W1': jax.random.normal(ks[4], (NUM_EXPERTS, D, 2 * D), jnp.float32) * s, 'b1': jnp.zeros((NUM_EXPERTS, 2 * D), jnp.float32), 'W2': jax.random.normal(ks[5], (NUM_EXPERTS, 2 * D, D), jnp.float32) * s, 'b2': jnp.zeros((NUM_EXPERTS, D), jnp.float32), 'edge_index': jax.random.randint(ks[6], (2, N_EDGES), 0, B * N, jnp.int32)}
    _L0_ffn_all = _L0_ffn_setup()
    _L0_ffn_in = {k: v for k, v in _L0_ffn_all.items() if k in ('W_gat', 'att_src', 'att_dst', 'b_gat', 'ln_gamma', 'ln_beta', 'W1', 'b1', 'W2', 'b2', 'edge_index')}
    del _L0_ffn_all
    return {'x': x, 'src': src, 'dst': dst, 'edge_attr_16': edge_attr_16, 'L0_gnn_W_l': _L0_gnn_in['W_l'], 'L0_gnn_b_l': _L0_gnn_in['b_l'], 'L0_gnn_W_r': _L0_gnn_in['W_r'], 'L0_gnn_b_r': _L0_gnn_in['b_r'], 'L0_gnn_W_e': _L0_gnn_in['W_e'], 'L0_gnn_att': _L0_gnn_in['att'], 'L0_gnn_bias': _L0_gnn_in['bias'], 'L0_ffn_W_gat': _L0_ffn_in['W_gat'], 'L0_ffn_att_src': _L0_ffn_in['att_src'], 'L0_ffn_att_dst': _L0_ffn_in['att_dst'], 'L0_ffn_b_gat': _L0_ffn_in['b_gat'], 'L0_ffn_ln_gamma': _L0_ffn_in['ln_gamma'], 'L0_ffn_ln_beta': _L0_ffn_in['ln_beta'], 'L0_ffn_W1': _L0_ffn_in['W1'], 'L0_ffn_b1': _L0_ffn_in['b1'], 'L0_ffn_W2': _L0_ffn_in['W2'], 'L0_ffn_b2': _L0_ffn_in['b2'], 'L0_ffn_edge_index': _L0_ffn_in['edge_index']}

def reference(x, src, dst, edge_attr_16, L0_gnn_W_l, L0_gnn_b_l, L0_gnn_W_r, L0_gnn_b_r, L0_gnn_W_e, L0_gnn_att, L0_gnn_bias, L0_ffn_W_gat, L0_ffn_att_src, L0_ffn_att_dst, L0_ffn_b_gat, L0_ffn_ln_gamma, L0_ffn_ln_beta, L0_ffn_W1, L0_ffn_b1, L0_ffn_W2, L0_ffn_b2, L0_ffn_edge_index):
    import jax
    import jax.numpy as jnp

    def _L0_gnn_ref(x, edge_index, edge_attr, W_l, b_l, W_r, b_r, W_e, att, bias):
        import jax, jax.numpy as jnp
        import numpy as np
        N, E = (6250, 50000)
        HEADS, DIMS, EDGE_DIM = (4, 64, 16)
        FEAT = HEADS * DIMS
        NEG_SLOPE = 0.2

        def _gatv2(x, edge_index, edge_attr, W_l, b_l, W_r, b_r, W_e, att, bias):
            n = x.shape[0]
            src, dst = (edge_index[0], edge_index[1])
            x_l = (x @ W_l.T + b_l).reshape(n, HEADS, DIMS)
            x_r = (x @ W_r.T + b_r).reshape(n, HEADS, DIMS)
            ones = jnp.ones((src.shape[0],), x.dtype)
            deg = jax.ops.segment_sum(ones, dst, num_segments=n)
            loop_attr = jax.ops.segment_sum(edge_attr, dst, num_segments=n)
            loop_attr = loop_attr / jnp.clip(deg, 1.0, None)[:, None]
            loop = jnp.arange(n, dtype=src.dtype)
            src = jnp.concatenate([src, loop])
            dst = jnp.concatenate([dst, loop])
            e_attr = jnp.concatenate([edge_attr, loop_attr], axis=0)
            e_feat = (e_attr @ W_e.T).reshape(-1, HEADS, DIMS)
            s = x_l[src] + x_r[dst] + e_feat
            s = jax.nn.leaky_relu(s, NEG_SLOPE)
            alpha = jnp.einsum('ehc,hc->eh', s, att)
            amax = jax.ops.segment_max(alpha, dst, num_segments=n)
            ex = jnp.exp(alpha - amax[dst])
            denom = jax.ops.segment_sum(ex, dst, num_segments=n)
            alpha = ex / (denom[dst] + 1e-16)
            out = jax.ops.segment_sum(alpha[..., None] * x_l[src], dst, num_segments=n)
            return out.reshape(n, FEAT) + bias
        h = _gatv2(x, edge_index, edge_attr, W_l, b_l, W_r, b_r, W_e, att, bias)
        h = jax.nn.silu(h)
        return x + h

    def _L0_ffn_ref(x, W_gat, att_src, att_dst, b_gat, ln_gamma, ln_beta, W1, b1, W2, b2, edge_index):
        import jax, jax.numpy as jnp
        import numpy as np
        B, N, D = (16, 512, 256)
        NUM_EXPERTS, TOP_K, HEADS = (4, 2, 4)
        N_EDGES = 131072
        LN_EPS = 1e-05

        def _layernorm(x, g, b):
            mu = x.mean(-1, keepdims=True)
            var = ((x - mu) ** 2).mean(-1, keepdims=True)
            return (x - mu) * jax.lax.rsqrt(var + LN_EPS) * g + b

        def _forward(x, edge_index, W_gat, att_src, att_dst, b_gat, ln_gamma, ln_beta, W1, b1, W2, b2):
            Bc, Nc, Dc = x.shape
            M = Bc * Nc
            x_flat = x.reshape(M, Dc)
            h = (x_flat @ W_gat).reshape(M, HEADS, NUM_EXPERTS)
            loops = jnp.arange(M, dtype=edge_index.dtype)
            src = jnp.concatenate([edge_index[0], loops])
            dst = jnp.concatenate([edge_index[1], loops])
            a_src = (h * att_src).sum(-1)
            a_dst = (h * att_dst).sum(-1)
            e = jax.nn.leaky_relu(a_src[src] + a_dst[dst], negative_slope=0.2)
            e_max = jax.ops.segment_max(e, dst, num_segments=M)
            ee = jnp.exp(e - e_max[dst])
            denom = jax.ops.segment_sum(ee, dst, num_segments=M)
            alpha = ee / (denom[dst] + 1e-16)
            msg = h[src] * alpha[:, :, None]
            agg = jax.ops.segment_sum(msg, dst, num_segments=M).reshape(M, HEADS * NUM_EXPERTS) + b_gat
            scores = _layernorm(agg, ln_gamma, ln_beta).reshape(M, HEADS, NUM_EXPERTS).mean(1)
            scores = scores.reshape(Bc, Nc, NUM_EXPERTS)
            topk_s, topk_i = jax.lax.top_k(scores, TOP_K)
            w = jax.nn.softmax(topk_s, axis=-1)
            out = jnp.zeros_like(x)
            for ei in range(NUM_EXPERTS):
                g = jnp.where(topk_i == ei, w, 0.0).sum(-1)
                hh = jax.nn.gelu(x @ W1[ei] + b1[ei], approximate=False)
                out = out + g[..., None] * (hh @ W2[ei] + b2[ei])
            return out
        return _forward(x, edge_index, W_gat, att_src, att_dst, b_gat, ln_gamma, ln_beta, W1, b1, W2, b2)
    edge_index = jnp.stack([src, dst])
    x = x + _L0_gnn_ref(_layernorm(x, axis=-1), edge_index, edge_attr_16, L0_gnn_W_l, L0_gnn_b_l, L0_gnn_W_r, L0_gnn_b_r, L0_gnn_W_e, L0_gnn_att, L0_gnn_bias)
    x = x + _L0_ffn_ref(_layernorm(x, axis=-1)[None], L0_ffn_W_gat, L0_ffn_att_src, L0_ffn_att_dst, L0_ffn_b_gat, L0_ffn_ln_gamma, L0_ffn_ln_beta, L0_ffn_W1, L0_ffn_b1, L0_ffn_W2, L0_ffn_b2, L0_ffn_edge_index)[0]
    return x

_drawn_inputs = setup_inputs


def setup_inputs(seed=0):
    import zlib

    import numpy as np

    out = dict(_drawn_inputs(seed))
    spreads = {'L0_gnn_b_l': (0.0, 0.1),
     'L0_gnn_b_r': (0.0, 2.0),
     'L0_gnn_bias': (0.0, 0.1),
     'L0_ffn_b_gat': (0.0, 0.1),
     'L0_ffn_ln_gamma': (1.0, 0.2),
     'L0_ffn_ln_beta': (0.0, 0.1),
     'L0_ffn_b1': (0.0, 0.303),
     'L0_ffn_b2': (0.0, 0.1)}
    factors = {'edge_attr_16': 7.021,
     'L0_gnn_W_r': 6.729,
     'L0_gnn_W_e': 7.925,
     'L0_gnn_att': 2.769,
     'L0_ffn_att_dst': 3.383}
    for name, (base, spread) in spreads.items():
        noise = np.random.default_rng([zlib.crc32(name.encode()), seed]).standard_normal(out[name].shape)
        drawn = base * np.exp(spread * noise) if base else spread * noise
        out[name] = jnp.asarray(drawn.astype(out[name].dtype))
    for name, factor in factors.items():
        out[name] = (out[name] * factor).astype(out[name].dtype)
    return out
```

```python
from contextlib import ExitStack

import concourse.bass as bass
from concourse import mybir

F32 = mybir.dt.float32
BF16 = mybir.dt.bfloat16
I32 = mybir.dt.int32
ALU = mybir.AluOpType
ACT = mybir.ActivationFunctionType
AX = mybir.AxisListType

P = 128
NODES, FEAT, HEADS, EDGE_DIM = 12500, 256, 4, 16
DIMS = FEAT // HEADS
BLOCKS = -(-NODES // P)
LAST_ROWS = NODES - (BLOCKS - 1) * P
NODES_PAD = BLOCKS * P
ZERO_ROW = NODES_PAD
EXPERTS, HIDDEN = 4, 512
GAT = HEADS * EXPERTS
NEG = -1.0e30
GROUP = 4
SLOTS = 3
SLOPE = 0.2
EPS = 1.0e-5


class Graph:

    def __init__(self, name, edges, rows, chunk, dims, width, words, extra):
        self.name, self.edges, self.rows, self.cols, self.chunk = name, edges, rows, edges // rows, chunk
        self.dims, self.width, self.words, self.extra = dims, width, words, extra
        self.sums = HEADS * (dims + 1)
        self.acc = self.sums + extra
        tiles = (edges + BLOCKS * (P - 1)) // P
        self.groups = -(-tiles // GROUP)
        self.tiles = self.groups * GROUP
        assert self.rows * self.cols == edges and self.cols % (2 * chunk) == 0


G1 = Graph("gnn", 200000, 125, 40, DIMS, HEADS * (DIMS + 1), 2 + EDGE_DIM + 1, EDGE_DIM + 1)
G2 = Graph("ffn", 131072, 128, 32, EXPERTS, HEADS * (EXPERTS + 1) + HEADS, 2, 0)


class Count:

    def __init__(self, engine, semaphore):
        self.engine, self.semaphore, self.value = engine, semaphore, 0

    def add(self, instruction):
        instruction.then_inc(self.semaphore, 1)
        self.value = self.value + 1

    def wait(self):
        self.engine.wait_ge(self.semaphore, self.value)

    def link(self, instruction):
        self.add(instruction)
        self.wait()


def settle(engine, s_settled):
    engine.sem_inc(s_settled, 1)


class Step:

    def __init__(self, k, o):
        self.k, self.o = k, o
        self.g = k * SLOTS + o
        self.slot = o % SLOTS
        self.uses = k + o // SLOTS

    def near(self, d):
        return Step(self.k, self.o + d)


def step_of(g):
    return Step(g // SLOTS, g % SLOTS)


def run_all(engine, groups, body):
    for g in range(SLOTS):
        body(step_of(g), True)
    runs = (groups - SLOTS) // SLOTS
    with engine.Fori(1, 1 + runs) as k:
        for o in range(SLOTS):
            body(Step(k, o), False)
    for g in range(SLOTS * (1 + runs), groups):
        body(step_of(g), False)


def run_groups(engine, groups, body):
    body(Step(0, 0), True, False)
    runs = (groups - 2) // SLOTS
    with engine.Fori(0, runs) as k:
        for o in range(SLOTS):
            body(Step(k, 1 + o), False, False)
    for g in range(1 + SLOTS * runs, groups):
        body(step_of(g), False, g == groups - 1)


def build(nc, x, src1, dst1, attr, w_lr, b_lr, w_e, att, bias, w_gat, att_src, att_dst, b_gat,
          ln_gamma, ln_beta, w1, b1, w2, b2, src2, dst2, out):
    ctx = ExitStack()
    with ctx:
        def sb(name, shape, dt=F32):
            return ctx.enter_context(nc.sbuf_tensor(name, shape, dt))

        def pb(name, shape, dt=F32):
            return ctx.enter_context(nc.psum_tensor(name, shape, dt))

        def sem(name):
            return ctx.enter_context(nc.semaphore(name))

        def dram(name, shape, dt=F32):
            return nc.dram_tensor(name, shape, dt, kind="Internal").ap()

        xl_table = dram("xl_table", [NODES_PAD + 1, G1.width])
        xr_table = dram("xr_table", [NODES_PAD, FEAT])
        xh_table = dram("xh_table", [NODES_PAD, FEAT])
        x1_table = dram("x1_table", [NODES_PAD, FEAT])
        gate_table = dram("gate_table", [NODES_PAD + 1, G2.width])
        adst_table = dram("adst_table", [NODES_PAD, HEADS])
        records = {G1: dram("records1", [P, G1.tiles * G1.words], I32),
                   G2: dram("records2", [P, G2.tiles * G2.words], I32)}
        gathered = {G1: xl_table, G2: gate_table}
        targets = {G1: (xr_table, FEAT), G2: (adst_table, HEADS)}

        arena = sb("arena", [P, BLOCKS * G1.acc])
        acc1 = arena[:, :].rearrange("p (b n) -> p b n", n=G1.acc)
        zT = acc1[:, :, 0:FEAT]
        acc2 = sb("acc2", [P, BLOCKS, G2.acc])
        max1 = sb("max1", [P, BLOCKS, HEADS])
        max2 = sb("max2", [P, BLOCKS, HEADS])
        accs, maxs = {G1: acc1, G2: acc2[:, :, :]}, {G1: max1, G2: max2}
        gate_rows = sb("gate_rows", [P, BLOCKS, G2.width])
        gate_flat = gate_rows[:, :, :].rearrange("p b n -> p (b n)")
        block_of = {G1: gate_flat[0:1, 0:G1.tiles].bitcast(I32), G2: sb("block_of2", [1, G2.tiles], I32)}

        ident = sb("ident", [P, P])
        ident_b = sb("ident_b", [P, P], BF16)
        before = sb("before", [P, P])
        ones = sb("ones", [P, P])
        iota = sb("iota", [P, P])
        wlr_sb = sb("wlr_sb", [P, 2, 2 * FEAT])
        blr_sb = sb("blr_sb", [1, 2 * FEAT])
        we_sb = sb("we_sb", [GROUP * G1.words, GROUP, FEAT])
        att_sb = sb("att_sb", [P, FEAT])
        bias_sb = sb("bias_sb", [P, FEAT])
        wgat_sb = sb("wgat_sb", [P, 2, GAT])
        gat_consts = sb("gat_consts", [P, 5, GAT])
        neg_half = sb("neg_half", [P, BLOCKS])

        at = [0]

        def part(width, dt=F32):
            lo = at[0]
            at[0] = lo + width
            assert at[0] <= BLOCKS * G1.acc
            a = arena[:, lo:lo + width]
            return a if dt == F32 else a.bitcast(dt)

        bucket = {}
        for g in (G1, G2):
            b = bucket[g] = {}
            for n, dt in (("dst", I32), ("src", I32), ("block", F32), ("within", F32)):
                b[n] = part(g.cols, dt)
            b["slot"] = b["dst"]
            b["rank"] = part(g.cols)
        hit, hits_so_far, picked = part(G1.cols), part(G1.tiles), part(G1.cols)
        hit_i, tile_i = hit.bitcast(I32), picked.bitcast(I32)
        passed = hits_so_far
        tile_iota_store = part(G1.tiles)
        counts = part(BLOCKS)
        tiles_of = part(BLOCKS)
        tiles_i = part(BLOCKS, I32)
        tile_end = part(BLOCKS)
        first_slot = part(BLOCKS)
        end_col = part(1)
        staged_slot = sb("staged_slot", [P, 2, G1.chunk], I32)
        staged_rec = sb("staged_rec", [P, 2, G1.chunk * G1.words], I32)
        staged_attr = sb("staged_attr", [P, 2, G1.chunk * EDGE_DIM])

        rec = sb("rec", [P, SLOTS, GROUP * G1.words], I32)
        WIDE = 10288
        wide = sb("wide", [P, WIDE])
        used = [0]

        def wide_part(*shape):
            size = 1
            for d in shape:
                size *= d
            lo = used[0]
            used[0] = lo + size
            assert used[0] <= WIDE
            names = " ".join(f"d{i}" for i in range(len(shape)))
            return wide[:, lo:lo + size].rearrange(f"p ({names}) -> p {names}",
                                                   **{f"d{i}": d for i, d in enumerate(shape)})

        tab = wide_part(SLOTS, GROUP * G1.width)
        trow = wide_part(SLOTS, GROUP * FEAT)
        oh = wide_part(SLOTS, GROUP, P)
        ohT = wide_part(SLOTS, GROUP, P)
        pen = sb("pen", [P, SLOTS, GROUP * P], BF16)
        attrT = sb("attrT", [GROUP * G1.words, SLOTS, P])
        relu = wide_part(GROUP * FEAT)
        lrelu = staged_attr[:, :, :].rearrange("p o n -> p (o n)")[:, 0:GROUP * FEAT]
        score = sb("score", [P, SLOTS, GROUP * HEADS])
        score_hi = sb("score_hi", [P, GROUP * HEADS], BF16)
        score_lo = sb("score_lo", [P, GROUP * HEADS], BF16)
        tmax = sb("tmax", [P, GROUP, HEADS])
        old_max = sb("old_max", [P, GROUP, HEADS])
        new_max = sb("new_max", [P, SLOTS, GROUP * HEADS])
        fall = sb("fall", [P, SLOTS, GROUP * HEADS])
        rescale = sb("rescale", [P, SLOTS, GROUP * HEADS])
        shifted = sb("shifted", [P, GROUP * HEADS])
        weight = sb("weight", [P, GROUP * HEADS])

        used[0] = 0
        nx = wide_part(2, FEAT)
        nh = wide_part(2, FEAT)
        nxh = wide_part(2, FEAT)
        nhT = wide_part(2, FEAT)
        nxl = wide_part(2, HEADS * (DIMS + 1))
        nxr = wide_part(2, FEAT)
        stats = sb("stats", [P, 6])
        mv = sb("mv", [P, 2])
        rstd = sb("rstd", [P, 2])
        small = sb("small", [P, 64])
        laT = sb("laT", [2 + EDGE_DIM, P])

        zg = acc1[:, :, FEAT:FEAT + GAT]
        adst = acc1[:, :, FEAT + GAT:FEAT + GAT + HEADS]

        banks = [pb(f"bank{n}", [P, 512]) for n in range(8)]

        s_const = sem("constants_made")
        s_settled = sem("settled")
        s_weights = sem("weights_loaded")
        s_dve = sem("vector_step_done")
        s_pool = sem("pool_step_done")
        s_act = sem("scalar_step_done")
        edges_loaded = {g: sem(f"edges_loaded_{g.name}") for g in (G1, G2)}
        s_bucket_mm = sem("bucket_product_done")
        s_bucket_in = sem("bucket_operand_ready")
        slots_ready = {g: sem(f"slots_ready_{g.name}") for g in (G1, G2)}
        blocks_ready = {g: sem(f"blocks_ready_{g.name}") for g in (G1, G2)}
        filler_made = sem("filler_made")
        filled = sem("records_filled")
        scattered = [sem("scattered_a"), sem("scattered_b")]
        all_scattered = {g: sem(f"all_scattered_{g.name}") for g in (G1, G2)}
        attr_loaded = [sem("attr_loaded_a"), sem("attr_loaded_b")]
        attr_used = sem("attr_used")

        block = ctx.enter_context(nc.Block())

        dve_n = {}

        def pool_constants(pool):
            n = Count(pool, s_pool)
            n.add(nc.gpsimd.memset(ident[:, :], 0.0))
            n.add(nc.gpsimd.memset(before[:, :], 1.0))
            n.link(nc.gpsimd.memset(neg_half[:, :], -0.5))
            nc.gpsimd.affine_select(out=ident[:, :], in_=ident[:, :], compare_op=ALU.not_equal, fill=1.0,
                                    base=0, pattern=[[-1, P]], channel_multiplier=1).then_inc(s_const, 1)
            nc.gpsimd.affine_select(out=before[:, :], in_=before[:, :], compare_op=ALU.is_gt, fill=0.0,
                                    base=0, pattern=[[1, P]], channel_multiplier=-1).then_inc(s_const, 1)
            nc.gpsimd.iota(iota[:, :], [[1, P]], base=0, channel_multiplier=0,
                           allow_small_or_imprecise_dtypes=True).then_inc(s_const, 1)
            nc.gpsimd.iota(tile_iota_store[:, :], [[1, G1.tiles]], base=0, channel_multiplier=0,
                           allow_small_or_imprecise_dtypes=True).then_inc(s_const, 1)
            return n

        def sync_weights(sp):
            sp.dma_start(wlr_sb[:, :, :], w_lr.rearrange("(k p) n -> p k n", p=P)).then_inc(s_weights, 16)
            sp.dma_start(blr_sb[:, :], b_lr).then_inc(s_weights, 16)
            sp.dma_start(wgat_sb[:, :, :], w_gat.rearrange("(k p) n -> p k n", p=P)).then_inc(s_weights, 16)
            sp.dma_start(att_sb[:, :], att.partition_broadcast(P)).then_inc(s_weights, 16)
            sp.dma_start(bias_sb[:, :], bias.partition_broadcast(P)).then_inc(s_weights, 16)
            for n, v in enumerate((att_src, att_dst, b_gat, ln_gamma, ln_beta)):
                sp.dma_start(gat_consts[:, n, :], v.partition_broadcast(P)).then_inc(s_weights, 16)
            sp.wait_ge(s_const, 6)
            for j in range(GROUP):
                sp.dma_start(we_sb[G1.words * j + 2:G1.words * j + 2 + EDGE_DIM, j, :], w_e).then_inc(s_weights, 16)

        WEIGHTS = 16 * (10 + GROUP)
        CONSTS = 8

        def sync_edges(sp, g, src, dst):
            b, r = bucket[g], g.rows
            sp.dma_start(b["dst"][0:r, :], dst.rearrange("(p c) -> p c", p=r)).then_inc(edges_loaded[g], 16)
            sp.dma_start(b["src"][0:r, :], src.rearrange("(p c) -> p c", p=r)).then_inc(edges_loaded[g], 16)

        def vector_buckets(v, g, n, first):
            b, r, c = bucket[g], g.rows, g.cols
            v.wait_ge(edges_loaded[g], 32)
            if first:
                v.wait_ge(s_const, CONSTS)
            n.add(nc.vector.tensor_scalar(tile_i[0:r, 0:c], b["dst"][0:r, :], 7, None, ALU.arith_shift_right))
            n.link(nc.vector.tensor_scalar(hit_i[0:r, 0:c], b["dst"][0:r, :], P - 1, None, ALU.bitwise_and))
            n.add(nc.vector.tensor_copy(b["block"][0:r, :], tile_i[0:r, 0:c]))
            n.add(nc.vector.tensor_copy(b["within"][0:r, :], hit_i[0:r, 0:c]))
            n.link(nc.vector.memset(b["rank"][0:r, :], 0.0))
            n0 = n.value
            with v.Fori(0, BLOCKS) as h:
                n.value = n0 + h
                n.link(nc.vector.tensor_scalar(hit[0:r, 0:c], b["block"][0:r, :], iota[0:r, bass.ds(h, 1)],
                                               0.0, ALU.is_equal, ALU.add,
                                               accum_out=counts[0:r, bass.ds(h, 1)]))
            n.value = n0 + BLOCKS
            nc.vector.tensor_copy(counts[0:1, 0:1], counts[0:1, 0:1]).then_inc(s_bucket_in, 1)
            k = 0 if first else 1
            v.wait_ge(s_bucket_mm, 4 * k + 1)
            n.link(nc.vector.tensor_scalar(tiles_i[:, :], banks[0][:, 0:BLOCKS], float(P - 1), None, ALU.add))
            n.link(nc.vector.tensor_scalar(tiles_i[:, :], tiles_i[:, :], 7, None, ALU.arith_shift_right))
            n.link(nc.vector.tensor_copy(tiles_of[:, :], tiles_i[:, :]))
            nc.vector.tensor_tensor_scan(tile_end[:, :], tiles_of[:, :], tiles_of[:, :], 0.0,
                                         ALU.add, ALU.max).then_inc(s_bucket_in, 1)
            v.wait_ge(s_bucket_in, 3 * k + 2)
            n.link(nc.vector.tensor_tensor(first_slot[:, :], tile_end[:, :], tiles_of[:, :], ALU.subtract))
            n.link(nc.vector.scalar_tensor_tensor(first_slot[:, :], first_slot[:, :], float(P),
                                                  banks[1][:, 0:BLOCKS], ALU.mult, ALU.add))
            v.wait_ge(s_bucket_mm, 4 * k + 2)
            n.link(nc.vector.tensor_copy(end_col[0:BLOCKS, :], banks[2][0:BLOCKS, 0:1]))
            nc.vector.tensor_scalar(passed[0:BLOCKS, 0:g.tiles], tile_iota_store[0:BLOCKS, 0:g.tiles],
                                    end_col[0:BLOCKS, 0:1], None, ALU.is_ge).then_inc(s_bucket_in, 1)
            v.wait_ge(s_bucket_mm, 4 * k + 3)
            for m, lo in enumerate(range(0, g.tiles, 512)):
                hi = min(g.tiles, lo + 512)
                nc.vector.tensor_scalar(block_of[g][0:1, lo:hi], banks[4 + m][0:1, 0:hi - lo],
                                        float(BLOCKS - 1), None, ALU.min).then_inc(blocks_ready[g], 1)
            n0 = n.value
            with v.Fori(0, BLOCKS) as h:
                n.value = n0 + h * 4
                n.link(nc.vector.tensor_scalar(hit[0:r, 0:c], b["block"][0:r, :], iota[0:r, bass.ds(h, 1)],
                                               None, ALU.is_equal))
                n.link(nc.vector.tensor_tensor_scan(hits_so_far[0:r, 0:c], hit[0:r, 0:c], hit[0:r, 0:c],
                                                    first_slot[0:r, bass.ds(h, 1)], ALU.add, ALU.max))
                n.link(nc.vector.tensor_tensor(picked[0:r, 0:c], hit[0:r, 0:c], hits_so_far[0:r, 0:c],
                                               ALU.mult))
                n.link(nc.vector.tensor_tensor(b["rank"][0:r, :], b["rank"][0:r, :], picked[0:r, 0:c],
                                               ALU.add))
            n.value = n0 + 4 * BLOCKS
            rank_i = b["slot"]
            n.link(nc.vector.tensor_scalar(rank_i[0:r, :], b["rank"][0:r, :], -1.0, None, ALU.add))
            n.add(nc.vector.tensor_scalar(tile_i[0:r, 0:c], rank_i[0:r, :], 7, None, ALU.arith_shift_right))
            n.link(nc.vector.tensor_scalar(hit_i[0:r, 0:c], rank_i[0:r, :], P - 1, None, ALU.bitwise_and))
            nc.vector.scalar_tensor_tensor(rank_i[0:r, :], hit_i[0:r, 0:c], float(g.tiles),
                                           tile_i[0:r, 0:c], ALU.mult, ALU.add).then_inc(slots_ready[g], 1)
            v.wait_ge(slots_ready[g], 1)

        def tensor_buckets(pe, g, k):
            r = g.rows
            pe.wait_ge(s_bucket_in, 3 * k + 1)
            nc.tensor.matmul(banks[0][:, 0:BLOCKS], ones[0:r, :], counts[0:r, :], start=True, stop=True)
            nc.tensor.matmul(banks[1][:, 0:BLOCKS], before[0:r, :], counts[0:r, :],
                             start=True, stop=True).then_inc(s_bucket_mm, 1)
            pe.wait_ge(s_bucket_in, 3 * k + 2)
            nc.tensor.transpose(banks[2][0:BLOCKS, 0:P], tile_end[:, :], ident[:, :]).then_inc(s_bucket_mm, 1)
            pe.wait_ge(s_bucket_in, 3 * k + 3)
            last = None
            for m, lo in enumerate(range(0, g.tiles, 512)):
                hi = min(g.tiles, lo + 512)
                last = nc.tensor.matmul(banks[4 + m][0:1, 0:hi - lo], ones[0:BLOCKS, 0:1],
                                        passed[0:BLOCKS, lo:hi], start=True, stop=True)
            last.then_inc(s_bucket_mm, 2)

        def sync_fill(sp):
            sp.wait_ge(filler_made, 2)
            for g in (G1, G2):
                per = g.tiles // 4 * g.words
                for q in range(4):
                    sp.dma_start(records[g][:, q * per:(q + 1) * per], filler(g)).then_inc(filled, 16)

        def filler(g):
            return fillers[g][:, 0:g.tiles // 4 * g.words]

        fillers = {G1: None, G2: None}
        zero_row = part(G1.width)[0:1, :]
        fillers[G1] = wide[:, 0:G1.tiles // 4 * G1.words].bitcast(I32)
        fillers[G2] = gate_flat[:, G1.tiles:G1.tiles + G2.tiles // 4 * G2.words].bitcast(I32)

        def pool_fill(pool, n):
            for g in (G1, G2):
                n.link(nc.gpsimd.memset(filler(g), 0))
            for g in (G1, G2):
                f = filler(g).rearrange("p (t w) -> p t w", w=g.words)
                n.link(nc.gpsimd.memset(f[:, :, 0:1], ZERO_ROW))
                nc.gpsimd.memset(f[:, :, 1:2].bitcast(F32), -1.0).then_inc(filler_made, 1)

        def sync_attr(sp, c0):
            g = G1
            a = attr.rearrange("(p c) d -> p (c d)", p=g.rows)
            w = g.chunk * EDGE_DIM
            chunks = g.cols // g.chunk

            def load(k, o):
                c = k * 2 + o
                sp.dma_start(staged_attr[0:g.rows, o, :], a[:, bass.ds(c * w, w)]).then_inc(attr_loaded[o], 16)
            load(0, 0)
            load(0, 1)
            with sp.Fori(1, chunks // 2) as k:
                for o in range(2):
                    sp.wait_ge(attr_used, k * 2 + (o - 1))
                    load(k, o)

        def pool_scatter(pool, g, base, n):
            b, r, ch, w = bucket[g], g.rows, g.chunk, g.words
            pool.wait_ge(slots_ready[g], 1)
            if g is G1:
                pool.wait_ge(filled, 16 * 8)
            out_rows = records[g].rearrange("p (t w) -> (p t) w", w=w)

            def chunk(k, o):
                c = (k * 2 + o) * ch
                pool.wait_ge(scattered[o], base + k * (16 * ch))
                settle(pool, s_settled)
                rv = staged_rec[0:r, o, 0:ch * w].rearrange("p (c w) -> p c w", w=w)
                rf = rv.bitcast(F32)

                def as3(a):
                    return a.rearrange("p (c w) -> p c w", w=1)
                nc.gpsimd.tensor_copy(staged_slot[0:r, o, 0:ch], b["slot"][0:r, bass.ds(c, ch)])
                nc.gpsimd.tensor_copy(rv[:, :, 0:1], as3(b["src"][0:r, bass.ds(c, ch)]))
                last = nc.gpsimd.tensor_copy(rf[:, :, 1:2], as3(b["within"][0:r, bass.ds(c, ch)]))
                n.link(last)
                settle(pool, s_settled)
                if g is G1:
                    pool.wait_ge(attr_loaded[o], k * 16 + 16)
                    settle(pool, s_settled)
                    nc.gpsimd.tensor_copy(
                        rf[:, :, 2:2 + EDGE_DIM],
                        staged_attr[0:r, o, :].rearrange("p (c d) -> p c d", d=EDGE_DIM)).then_inc(attr_used, 1)
                    pool.wait_ge(attr_used, k * 2 + (o + 1))
                    settle(pool, s_settled)
                for j in range(ch):
                    nc.gpsimd.indirect_dma_start(
                        out=out_rows, out_offset=bass.IndirectOffsetOnAxis(ap=staged_slot[0:r, o, j:j + 1], axis=0),
                        in_=staged_rec[0:r, o, j * w:(j + 1) * w], in_offset=None).then_inc(scattered[o], 16)

            if g is G1:
                for o in range(2):
                    rv = staged_rec[:, o, :].rearrange("p (c w) -> p c w", w=w)
                    n.link(nc.gpsimd.memset(rv[:, :, w - 1:w].bitcast(F32), 1.0))
            n0 = n.value
            with pool.Fori(0, g.cols // (2 * ch)) as k:
                n.value = n0 + k * 2
                chunk(k, 0)
                chunk(k, 1)
            n.value = n0 + g.cols // ch
            done = base + 16 * (g.cols // 2)
            for o in range(2):
                pool.wait_ge(scattered[o], done)
            pool.sem_inc(all_scattered[g], 1)
            return done

        x_loaded = [sem("x_loaded_a"), sem("x_loaded_b")]
        x_tile_free = sem("x_tile_free")
        h_ready = sem("h_ready")
        hT_in_psum = sem("hT_in_psum")
        hT_ready = sem("hT_ready")
        lr_in_psum = sem("lr_in_psum")
        lr_ready = sem("lr_ready")
        node_stored = [sem("node_stored_a"), sem("node_stored_b")]
        rstd_in = sem("variance_ready")
        rstd_out = sem("rstd_ready")
        nxl_made = sem("nxl_made")

        def run_blocks(engine, body):
            with engine.Fori(0, BLOCKS // 2 - 1) as k:
                body(k, 0, P)
                body(k, 1, P)
            k = BLOCKS // 2 - 1
            body(k, 0, P)
            body(k, 1, LAST_ROWS)

        def rows_of(table, k, o, rows=P):
            return table[bass.ds(k * (2 * P) + o * P, rows), :]

        def sync_nodes(sp):
            def body(k, o, rows):
                b = k * 2 + o
                sp.wait_ge(x_tile_free, b + 1)
                sp.dma_start(nx[0:rows, o, :], rows_of(x, k, o, rows)).then_inc(x_loaded[o], 16)
            run_blocks(sp, body)

        def scalar_nodes(act, n):
            def body(k, o, rows):
                b = k * 2 + o
                act.wait_ge(hT_in_psum, b + 1)
                nc.scalar.copy(nhT[:, o, :], banks[o][:, 0:FEAT]).then_inc(hT_ready, 1)
                act.wait_ge(lr_in_psum, b + 1)
                act.wait_ge(node_stored[o], k * 48)
                nc.scalar.copy(nxl[:, o, :].rearrange("p (h d) -> p h d", h=HEADS)[:, :, 0:DIMS],
                               banks[2 + o][:, 0:FEAT].rearrange("p (h d) -> p h d", h=HEADS)).then_inc(lr_ready, 1)
                nc.scalar.copy(nxr[:, o, :], banks[2 + o][:, FEAT:2 * FEAT]).then_inc(lr_ready, 1)
                act.wait_ge(lr_ready, b * 2 + 2)
                act.dma_start(rows_of(xl_table, k, o), nxl[:, o, :]).then_inc(node_stored[o], 16)
                act.dma_start(rows_of(xr_table, k, o), nxr[:, o, :]).then_inc(node_stored[o], 16)
                act.wait_ge(h_ready, b * 2 + 2)
                act.dma_start(rows_of(xh_table, k, o), nxh[:, o, :]).then_inc(node_stored[o], 16)
            act.wait_ge(nxl_made, 2)
            run_blocks(act, body)

        NODE_STORES = 48 * (BLOCKS // 2)

        def vector_nodes(v, n):
            v.wait_ge(filled, 16 * 8)
            nc.vector.memset(nxl[:, 0, :], 1.0).then_inc(nxl_made, 1)
            nc.vector.memset(nxl[:, 1, :], 1.0).then_inc(nxl_made, 1)
            nc.vector.memset(nx[:, 0, :], 0.0).then_inc(x_tile_free, 1)
            nc.vector.memset(nx[:, 1, :], 0.0).then_inc(x_tile_free, 1)
            base = [n.value]
            LINKS = 3

            def body(k, o, rows):
                b = k * 2 + o
                n.value = base[0] + b * LINKS
                v.wait_ge(x_loaded[o], k * 16 + 16)
                n.link(nc.vector.bn_stats(stats[:, :], nx[:, o, :]))
                settle(v, s_settled)
                n.link(nc.vector.bn_aggr(mv[:, :], stats[:, :]))
                nc.vector.tensor_scalar(rstd[:, 0:1], mv[:, 1:2], EPS, None, ALU.add).then_inc(rstd_in, 1)
                v.wait_ge(rstd_out, b + 1)
                v.wait_ge(hT_in_psum, b)
                v.wait_ge(node_stored[o], k * 48)
                nc.vector.tensor_scalar(nh[:, o, :], nx[:, o, :], mv[:, 0:1], rstd[:, 1:2],
                                        ALU.subtract, ALU.mult).then_inc(h_ready, 1)
                v.wait_ge(h_ready, b * 2 + 1)
                nc.vector.tensor_tensor(nxh[:, o, :], nx[:, o, :], nh[:, o, :], ALU.add).then_inc(h_ready, 1)
                n.link(nc.vector.memset(stats[:, :], 0.0))
                if not isinstance(k, int) or k < BLOCKS // 2 - 1:
                    nc.vector.memset(nx[:, o, :], 0.0).then_inc(x_tile_free, 1)
            run_blocks(v, body)
            n.value = base[0] + LINKS * BLOCKS

        def pool_rstd(pool, count, base=0):
            with pool.Fori(0, count) as i:
                pool.wait_ge(rstd_in, i + (base + 1))
                nc.gpsimd.tensor_tensor(rstd[:, 1:2], rstd[:, 0:1], neg_half[:, 0:1], ALU.pow).then_inc(rstd_out, 1)

        def tensor_nodes(pe):
            def body(k, o, rows):
                b = k * 2 + o
                pe.wait_ge(h_ready, b * 2 + 1)
                pe.wait_ge(hT_ready, b)
                for q in range(2):
                    last = nc.tensor.transpose(banks[o][:, q * P:(q + 1) * P], nh[:, o, q * P:(q + 1) * P],
                                               ident[:, :])
                last.then_inc(hT_in_psum, 1)
                pe.wait_ge(hT_ready, b + 1)
                pe.wait_ge(lr_ready, b * 2)
                for q in range(2):
                    nc.tensor.matmul(banks[2 + o][:, :], nhT[:, o, q * P:(q + 1) * P], wlr_sb[:, q, :],
                                     start=(q == 0), stop=False)
                nc.tensor.matmul(banks[2 + o][:, :], ones[0:1, :], blr_sb[0:1, :],
                                 start=False, stop=True).then_inc(lr_in_psum, 1)
            pe.wait_ge(s_weights, WEIGHTS)
            run_blocks(pe, body)

        class Signals:
            def __init__(self, g):
                def s(name):
                    return sem(f"{name}_{g.name}")
                self.rec = [s(f"records_{o}") for o in range(SLOTS)]
                self.trow = [s(f"target_rows_{o}") for o in range(SLOTS)]
                self.tab = [s(f"gathered_{o}") for o in range(SLOTS)]
                self.onehot, self.ohT_psum, self.ohT = s("onehot"), s("onehotT_in_psum"), s("onehotT_ready")
                self.s_psum, self.relu, self.s_used = s("sum_in_psum"), s("relu_ready"), s("sum_used")
                self.split, self.m_psum, self.m_read = s("score_split"), s("masked_in_psum"), s("masked_read")
                self.new_max, self.me_psum, self.shifted = s("new_max"), s("edge_max_in_psum"), s("shifted")
                self.weight, self.rescale, self.pay = s("weight"), s("rescale"), s("weighted")
                self.agg_psum, self.agg_read = s("aggregate_in_psum"), s("aggregate_read")
                self.score = s("score_ready")

        sig = {}
        OHT, MISC = banks[0], banks[1]
        SUM, MASKED, AGG = banks[2:4], banks[4:6], banks[6:8]
        EDGE_MAX = MISC[:, 256:256 + GROUP * HEADS]

        def register_blocks(engine, g, step):
            _, regs = nc.values_load_multi_w_load_instructions(
                block_of[g][0:1, bass.ds(step.g * GROUP, GROUP)], engines=[engine], min_val=0,
                max_val=BLOCKS - 1, skip_runtime_bounds_check_because="block_of is at most BLOCKS - 1")
            return regs

        def sync_edges_loop(sp, g):
            s, (table, width) = sig[g], targets[g]

            def load(step, first):
                o = step.slot
                if not first:
                    sp.wait_ge(s.agg_psum, (step.g - (SLOTS - 1)) * GROUP)
                sp.dma_start(rec[:, o, 0:GROUP * g.words],
                             records[g][:, bass.ds(step.g * (GROUP * g.words), GROUP * g.words)]).then_inc(s.rec[o], 16)
                regs = register_blocks(mybir.EngineType.SP, g, step)
                if not first:
                    sp.wait_ge(s.s_psum, (step.g - (SLOTS - 1)) * 2)
                for j in range(GROUP):
                    sp.dma_start(trow[:, o, j * width:(j + 1) * width],
                                 table[bass.ds(regs[j] * P, P), :]).then_inc(s.trow[o], 16)
            run_all(sp, g.groups, load)

        def pool_edges_loop(pool, g):
            s = sig[g]

            def gather(step, first):
                o, u = step.slot, step.uses
                pool.wait_ge(s.rec[o], u * 16 + 16)
                if not first:
                    pool.wait_ge(s.agg_psum, (step.g - (SLOTS - 1)) * GROUP)
                    settle(pool, s_settled)
                for j in range(GROUP):
                    nc.gpsimd.indirect_dma_start(
                        out=tab[:, o, j * g.width:(j + 1) * g.width], out_offset=None, in_=gathered[g],
                        in_offset=bass.IndirectOffsetOnAxis(ap=rec[:, o, j * g.words:j * g.words + 1], axis=0)
                    ).then_inc(s.tab[o], 16)
            run_all(pool, g.groups, gather)

        def tensor_edges_loop(pe, g):
            s = sig[g]
            is1 = g is G1
            width = targets[g][1]

            def transposes(t):
                o = t.slot
                pe.wait_ge(s.onehot, t.g + 1)
                if not (isinstance(t.g, int) and t.g == 0):
                    pe.wait_ge(s.ohT, t.g * (3 if is1 else 2))
                for j in range(GROUP):
                    last = nc.tensor.transpose(OHT[:, j * P:(j + 1) * P], oh[:, o, j, :], ident[:, :])
                if is1:
                    last = nc.tensor.transpose(MISC[0:GROUP * g.words, 0:P],
                                               rec[:, o, 0:GROUP * g.words].bitcast(F32), ident[:, :])
                last.then_inc(s.ohT_psum, 1)

            def sums(t):
                o = t.slot
                pe.wait_ge(s.ohT, (t.g + 1) * (3 if is1 else 2))
                pe.wait_ge(s.trow[o], t.uses * 64 + 64)
                pe.wait_ge(s.tab[o], t.uses * 64 + 64)
                if not (isinstance(t.g, int) and t.g == 0):
                    pe.wait_ge(s.s_used, t.g)
                for j in range(GROUP):
                    dst = SUM[j // 2][:, (j % 2) * FEAT:(j % 2) * FEAT + width]
                    row = tab[:, o, j * g.width:(j + 1) * g.width]
                    nc.tensor.matmul(dst, ohT[:, o, j, :], trow[:, o, j * width:(j + 1) * width],
                                     start=True, stop=False)
                    if is1:
                        nc.tensor.matmul(dst, attrT[:, o, :], we_sb[:, j, :], start=False, stop=False)
                        row = row.rearrange("p (h d) -> p h d", h=HEADS)[:, :, 0:DIMS]
                    else:
                        row = row[:, g.sums:g.sums + HEADS]
                    last = nc.tensor.matmul(dst, ident[:, :], row, start=False, stop=True)
                    if j % 2:
                        last.then_inc(s.s_psum, 1)

            def masked(t):
                o = t.slot
                pe.wait_ge(s.split, t.g + 1)
                for j in range(GROUP):
                    bank = MASKED[j % 2]
                    if not (isinstance(t.g, int) and t.g == 0 and j < 2):
                        pe.wait_ge(s.m_read, t.g * GROUP + (j - 1))
                    pj = pen[:, o, j * P:(j + 1) * P]
                    for h in range(HEADS):
                        nc.tensor.matmul(bank[:, h * P:(h + 1) * P], ident_b[:, :], pj, start=True, stop=False)
                        for half in (score_hi, score_lo):
                            c = j * HEADS + h
                            last = nc.tensor.matmul(bank[:, h * P:(h + 1) * P],
                                                    half[:, c:c + 1].broadcast_to([P, P]), ident_b[:, :],
                                                    start=False, stop=(half is score_lo))
                    last.then_inc(s.m_psum, 1)

            def edge_max(t):
                o = t.slot
                pe.wait_ge(s.new_max, t.g + 1)
                if not (isinstance(t.g, int) and t.g == 0):
                    pe.wait_ge(s.shifted, t.g)
                for j in range(GROUP):
                    c = slice(j * HEADS, (j + 1) * HEADS)
                    last = nc.tensor.matmul(EDGE_MAX[:, c], ohT[:, o, j, :], new_max[:, o, c], start=True, stop=True)
                last.then_inc(s.me_psum, 1)

            def aggregate(t):
                o = t.slot
                pe.wait_ge(s.pay, t.g + 1)
                for j in range(GROUP):
                    pe.wait_ge(s.agg_read, t.g * GROUP + (j + 1))
                    last = nc.tensor.matmul(AGG[j % 2][:, 0:g.sums], oh[:, o, j, :],
                                            tab[:, o, j * g.width:j * g.width + g.sums], start=True, stop=True)
                    if is1:
                        e = rec[:, o, j * g.words + 2:(j + 1) * g.words].bitcast(F32)
                        last = nc.tensor.matmul(AGG[j % 2][:, g.sums:g.acc], oh[:, o, j, :], e,
                                                start=True, stop=True, skip_group_check=True)
                    last.then_inc(s.agg_psum, 1)

            def body(t, first, last):
                if not last:
                    transposes(t.near(1))
                masked(t)
                if not first:
                    aggregate(t.near(-1))
                if not last:
                    sums(t.near(1))
                edge_max(t)
            transposes(Step(0, 0))
            sums(Step(0, 0))
            run_groups(pe, g.groups, body)
            aggregate(step_of(g.groups - 1))

        def scalar_edges_loop(act, g):
            s = sig[g]
            is1 = g is G1

            def copies(t):
                o = t.slot
                act.wait_ge(s.ohT_psum, t.g + 1)
                if not (isinstance(t.g, int) and t.g < SLOTS):
                    act.wait_ge(s.me_psum, t.g - (SLOTS - 1))
                nc.scalar.copy(ohT[:, o, :, :].rearrange("p j e -> p (j e)"), OHT[:, :]).then_inc(s.ohT, 1)
                nc.scalar.activation(pen[:, o, :], OHT[:, :], ACT.Copy, bias=NEG, scale=-NEG).then_inc(s.ohT, 1)
                if is1:
                    nc.scalar.copy(attrT[:, o, :], MISC[0:GROUP * G1.words, 0:P]).then_inc(s.ohT, 1)

            def relus(t):
                if is1:
                    for q in range(2):
                        act.wait_ge(s.s_psum, t.g * 2 + (q + 1))
                        nc.scalar.activation(relu[:, q * 512:(q + 1) * 512], SUM[q][:, :], ACT.Relu,
                                             scale=1.0 - SLOPE).then_inc(s.relu, 1)
                else:
                    act.wait_ge(s.s_psum, t.g * 2 + 2)
                    for q in range(2):
                        nc.scalar.activation(
                            relu[:, q * 8:(q + 1) * 8].rearrange("p (j h) -> p j h", h=HEADS),
                            SUM[q][:, :].rearrange("p (j f) -> p j f", f=FEAT)[:, :, 0:HEADS], ACT.Relu,
                            scale=1.0 - SLOPE).then_inc(s.relu, 1)

            def weights(t):
                act.wait_ge(s.shifted, t.g + 1)
                nc.scalar.activation(weight[:, :], shifted[:, :], ACT.Exp).then_inc(s.weight, 1)

            def rescales(t):
                act.wait_ge(s.new_max, t.g + 1)
                nc.scalar.activation(rescale[:, t.slot, :], fall[:, t.slot, :], ACT.Exp).then_inc(s.rescale, 1)

            def body(t, first, last):
                if not first:
                    weights(t.near(-1))
                if not last:
                    copies(t.near(1))
                    relus(t.near(1))
                rescales(t)
            copies(Step(0, 0))
            relus(Step(0, 0))
            run_groups(act, g.groups, body)
            weights(step_of(g.groups - 1))

        def vector_edges_loop(v, g, n):
            s = sig[g]
            is1 = g is G1
            acc, mx = accs[g], maxs[g]
            LINKS = 2 + 1 + GROUP + (1 if is1 else 0) + (0 if is1 else GROUP) + GROUP
            base = [n.value]

            def onehots(t):
                o = t.slot
                v.wait_ge(s.rec[o], t.uses * 16 + 16)
                if not (isinstance(t.g, int) and t.g < SLOTS):
                    v.wait_ge(s.agg_psum, (t.g - (SLOTS - 1)) * GROUP)
                w = rec[:, o, 0:GROUP * g.words].bitcast(F32).rearrange("p (j w) -> p j w", w=g.words)[:, :, 1:2]
                nc.vector.tensor_tensor(oh[:, o, :, :], iota[:, :].unsqueeze(1).broadcast_to([P, GROUP, P]),
                                        w.broadcast_to([P, GROUP, P]), ALU.is_equal).then_inc(s.onehot, 1)

            def shift(t):
                v.wait_ge(s.me_psum, t.g + 1)
                nc.vector.tensor_tensor(shifted[:, :], score[:, t.slot, :], EDGE_MAX, ALU.subtract).then_inc(s.shifted, 1)

            def scores(t):
                o = t.slot
                v.wait_ge(s.relu, t.g * 2 + 2)
                sc = score[:, o, :]
                if is1:
                    for q in range(2):
                        c = slice(q * 512, (q + 1) * 512)
                        last = nc.vector.scalar_tensor_tensor(lrelu[:, c], SUM[q][:, :], SLOPE, relu[:, c],
                                                              ALU.mult, ALU.add)
                    last.then_inc(s.s_used, 1)
                    v.wait_ge(s.s_used, t.g + 1)
                    l4 = lrelu[:, :].rearrange("p (j f) -> p j f", f=FEAT)
                    n.link(nc.vector.tensor_tensor(l4, l4, att_sb[:, :].unsqueeze(1).broadcast_to([P, GROUP, FEAT]),
                                                   ALU.mult))
                    nc.vector.tensor_reduce(sc, lrelu[:, :].rearrange("p (c d) -> p c d", d=DIMS), AX.X,
                                            ALU.add).then_inc(s.score, 1)
                else:
                    for q in range(2):
                        last = nc.vector.scalar_tensor_tensor(
                            sc[:, q * 8:(q + 1) * 8].rearrange("p (j h) -> p j h", h=HEADS),
                            SUM[q][:, :].rearrange("p (j f) -> p j f", f=FEAT)[:, :, 0:HEADS], SLOPE,
                            relu[:, q * 8:(q + 1) * 8].rearrange("p (j h) -> p j h", h=HEADS), ALU.mult, ALU.add)
                        last.then_inc(s.s_used if q else s.score, 1)
                    v.wait_ge(s.s_used, t.g + 1)
                v.wait_ge(s.score, t.g + 1)
                if not (isinstance(t.g, int) and t.g == 0):
                    v.wait_ge(s.m_psum, t.g * GROUP)
                n.link(nc.vector.tensor_copy(score_hi[:, :], sc))
                nc.vector.tensor_tensor(score_lo[:, :], sc, score_hi[:, :], ALU.subtract).then_inc(s.split, 1)

            def weighted(t):
                o = t.slot
                v.wait_ge(s.weight, t.g + 1)
                rows = tab[:, o, 0:GROUP * g.width].rearrange("p (j w) -> p j w", w=g.width)[:, :, 0:g.sums]
                rows = rows.rearrange("p j (h d) -> p j h d", h=HEADS)
                wt = weight[:, :].rearrange("p (j h) -> p j h", h=HEADS).unsqueeze(3).broadcast_to(
                    [P, GROUP, HEADS, g.dims + 1])
                nc.vector.tensor_tensor(rows, rows, wt, ALU.mult).then_inc(s.pay, 1)

            def tile_max(t):
                for j in range(GROUP):
                    v.wait_ge(s.m_psum, t.g * GROUP + (j + 1))
                    nc.vector.tensor_reduce(tmax[:, j, :], MASKED[j % 2][:, :].rearrange("p (h e) -> p h e", h=HEADS),
                                            AX.X, ALU.max).then_inc(s.m_read, 1)

            def accumulate(t):
                regs = register_blocks(mybir.EngineType.DVE, g, t)
                o = t.slot
                v.wait_ge(s.rescale, t.g + 1)
                for j in range(GROUP):
                    v.wait_ge(s.agg_psum, t.g * GROUP + (j + 1))
                    a = acc[:, bass.ds(regs[j], 1), :].rearrange("p a n -> p (a n)")
                    bank = AGG[j % 2]
                    if is1:
                        w = g.dims + 1
                        for h in range(HEADS):
                            c = slice(h * w, (h + 1) * w)
                            r = rescale[:, o, j * HEADS + h:j * HEADS + h + 1]
                            nc.vector.scalar_tensor_tensor(a[:, c], a[:, c], r, bank[:, c], ALU.mult, ALU.add)
                        c = slice(g.sums, g.acc)
                        last = nc.vector.tensor_tensor(a[:, c], a[:, c], bank[:, c], ALU.add)
                    else:
                        r = rescale[:, o, j * HEADS:(j + 1) * HEADS].unsqueeze(2).broadcast_to([P, HEADS, g.dims + 1])
                        a3 = a.rearrange("p (h d) -> p h d", h=HEADS)
                        n.link(nc.vector.tensor_tensor(a3, a3, r, ALU.mult))
                        last = nc.vector.tensor_tensor(a, a, bank[:, 0:g.sums], ALU.add)
                    last.then_inc(s.agg_read, 1)
                    v.wait_ge(s.agg_read, t.g * GROUP + (j + 3))

            def maxima(t):
                o = t.slot
                regs = register_blocks(mybir.EngineType.DVE, g, t)
                v.wait_ge(s.m_read, t.g * GROUP + GROUP)
                if not (isinstance(t.g, int) and t.g < 2):
                    v.wait_ge(s.me_psum, t.g - 1)
                    v.wait_ge(s.rescale, t.g - 1)
                for j in range(GROUP):
                    m = mx[:, bass.ds(regs[j], 1), :].rearrange("p a n -> p (a n)")
                    nm = new_max[:, o, j * HEADS:(j + 1) * HEADS]
                    nc.vector.tensor_copy(old_max[:, j, :], m)
                    nc.vector.tensor_tensor(nm, m, tmax[:, j, :], ALU.max)
                    n.link(nc.vector.tensor_tensor(m, m, tmax[:, j, :], ALU.max))
                nc.vector.tensor_tensor(fall[:, o, :], old_max[:, :, :].rearrange("p j h -> p (j h)"),
                                        new_max[:, o, :], ALU.subtract).then_inc(s.new_max, 1)

            PER = (2 if is1 else 1) + (0 if is1 else GROUP) + GROUP

            def body(t, first, last):
                if first:
                    n.value = base[0]
                else:
                    n.value = base[0] + (PER - (0 if is1 else GROUP)) + (t.g - 1) * PER
                if not first:
                    shift(t.near(-1))
                if not last:
                    onehots(t.near(1))
                scores(t)
                if not first:
                    weighted(t.near(-1))
                tile_max(t)
                if not first:
                    accumulate(t.near(-1))
                maxima(t)
            v.sem_inc(s.agg_read, 2)
            onehots(Step(0, 0))
            run_groups(v, g.groups, body)
            t = step_of(g.groups - 1)
            shift(t)
            weighted(t)
            accumulate(t)
            n.value = base[0] + PER * g.groups

        fin_free = sem("node_buffers_free")
        fin_loaded = [sem("node_rows_loaded_a"), sem("node_rows_loaded_b")]
        mean_attr, mean_attr_psum, mean_attr_T = sem("mean_attr"), sem("mean_attr_in_psum"), sem("mean_attr_T")
        self_sum = sem("self_attr_in_psum")
        self_fall, self_exp = sem("self_fall"), sem("self_exp")
        neg_out, exp_out = sem("layer_output"), sem("exp_of_output")
        x1_ready, x1_stored = sem("x1_ready"), [sem("x1_stored_a"), sem("x1_stored_b")]
        z_ready, z_psum, z_copied = sem("z_ready"), sem("z_in_psum"), sem("z_copied")
        zg_psum, zg_copied = sem("zg_in_psum"), sem("zg_copied")
        gate_rows_ready, gate_rows_stored = sem("gate_rows_ready"), sem("gate_rows_stored")
        GATE_STORES = 32

        def sync_finish(sp):
            def body(k, o, rows):
                sp.wait_ge(fin_free, k * 2 + (o + 1))
                sp.dma_start(nxl[:, o, :], rows_of(xl_table, k, o)).then_inc(fin_loaded[o], 16)
                sp.dma_start(nxr[:, o, :], rows_of(xr_table, k, o)).then_inc(fin_loaded[o], 16)
                sp.dma_start(nxh[:, o, :], rows_of(xh_table, k, o)).then_inc(fin_loaded[o], 16)
            run_blocks(sp, body)
            sp.wait_ge(gate_rows_ready, 1)
            sp.dma_start(gate_table[0:NODES_PAD, :].rearrange("(b p) w -> p b w", p=P),
                         gate_rows[:, :, :]).then_inc(gate_rows_stored, 16)
            sp.dma_start(adst_table[:, :].rearrange("(b p) w -> p b w", p=P), adst).then_inc(gate_rows_stored, 16)

        def scalar_finish(act):
            def body(k, o, rows):
                b = k * 2 + o
                act.wait_ge(mean_attr_psum, b + 1)
                nc.scalar.copy(laT[:, :], banks[o][0:2 + EDGE_DIM, 0:P]).then_inc(mean_attr_T, 1)
                act.wait_ge(self_fall, b + 1)
                nc.scalar.activation(small[:, 40:48], small[:, 32:40], ACT.Exp).then_inc(self_exp, 1)
                act.wait_ge(neg_out, b + 1)
                nc.scalar.activation(nx[:, o, :], nh[:, o, :], ACT.Exp, scale=-1.0).then_inc(exp_out, 1)
                act.wait_ge(x1_ready, b + 1)
                act.dma_start(rows_of(x1_table, k, o), nh[:, o, :]).then_inc(x1_stored[o], 16)
                act.wait_ge(z_psum, b + 1)
                nc.scalar.copy(nhT[:, o, :], banks[o][:, 0:FEAT]).then_inc(z_copied, 1)
                nc.scalar.copy(zT[:, bass.ds(b, 1), :].rearrange("p a n -> p (a n)"),
                               banks[o][:, 0:FEAT]).then_inc(z_copied, 1)
                act.wait_ge(zg_psum, b + 1)
                nc.scalar.copy(zg[:, bass.ds(b, 1), :].rearrange("p a n -> p (a n)"),
                               banks[4 + o][:, 0:GAT]).then_inc(zg_copied, 1)
            run_blocks(act, body)

        def tensor_finish(pe):
            def body(k, o, rows):
                b = k * 2 + o
                pe.wait_ge(mean_attr, b + 1)
                nc.tensor.transpose(banks[o][0:2 + EDGE_DIM, 0:P], small[:, 0:2 + EDGE_DIM],
                                    ident[:, :]).then_inc(mean_attr_psum, 1)
                pe.wait_ge(mean_attr_T, b + 1)
                nc.tensor.matmul(banks[2 + o][:, 0:FEAT], laT[:, :], we_sb[0:2 + EDGE_DIM, 0, :],
                                 start=True, stop=True).then_inc(self_sum, 1)
                pe.wait_ge(z_ready, b + 1)
                for q in range(2):
                    last = nc.tensor.transpose(banks[o][:, q * P:(q + 1) * P], nx[:, o, q * P:(q + 1) * P], ident[:, :])
                last.then_inc(z_psum, 1)
                pe.wait_ge(z_copied, b * 2 + 2)
                for q in range(2):
                    last = nc.tensor.matmul(banks[4 + o][:, 0:GAT], nhT[:, o, q * P:(q + 1) * P], wgat_sb[:, q, :],
                                            start=(q == 0), stop=(q == 1))
                last.then_inc(zg_psum, 1)
            run_blocks(pe, body)

        def vector_finish(v, n):
            base = [n.value]
            LINKS = 20

            def heads(a):
                return a.rearrange("p (h d) -> p h d", h=HEADS)

            def body(k, o, rows):
                b = k * 2 + o
                n0 = base[0] + b * LINKS
                n.value = n0
                a = acc1[:, bass.ds(b, 1), :].rearrange("p a n -> p (a n)")
                m = max1[:, bass.ds(b, 1), :].rearrange("p a n -> p (a n)")
                xl, xr, xh, s = nxl[:, o, :], nxr[:, o, :], nxh[:, o, :], nh[:, o, :]
                n.link(nc.vector.tensor_scalar(small[:, 20:21], a[:, G1.acc - 1:G1.acc], 1.0, None, ALU.max))
                n.link(nc.vector.reciprocal(small[:, 21:22], small[:, 20:21]))
                nc.vector.tensor_scalar(small[:, 2:2 + EDGE_DIM], a[:, G1.sums:G1.sums + EDGE_DIM],
                                        small[:, 21:22], None, ALU.mult).then_inc(mean_attr, 1)
                v.wait_ge(fin_loaded[o], k * 48 + 48)
                v.wait_ge(self_sum, b + 1)
                v.wait_ge(x1_stored[o], k * 16)
                n.link(nc.vector.tensor_tensor(s, banks[2 + o][:, 0:FEAT], xr, ALU.add))
                n.link(nc.vector.tensor_tensor(heads(s), heads(s), heads(xl)[:, :, 0:DIMS], ALU.add))
                n.link(nc.vector.scalar_tensor_tensor(s, s, SLOPE, s, ALU.mult, ALU.max))
                n.link(nc.vector.tensor_tensor(s, s, att_sb[:, :], ALU.mult))
                n.link(nc.vector.tensor_reduce(small[:, 24:28], heads(s), AX.X, ALU.add))
                n.link(nc.vector.tensor_tensor(small[:, 28:32], m, small[:, 24:28], ALU.max))
                n.add(nc.vector.tensor_tensor(small[:, 32:36], m, small[:, 28:32], ALU.subtract))
                nc.vector.tensor_tensor(small[:, 36:40], small[:, 24:28], small[:, 28:32],
                                        ALU.subtract).then_inc(self_fall, 1)
                v.wait_ge(self_exp, b + 1)

                def per_head(c, width):
                    return small[:, c:c + HEADS].unsqueeze(2).broadcast_to([P, HEADS, width])
                a4 = heads(a[:, 0:G1.sums])
                n.add(nc.vector.tensor_tensor(a4, a4, per_head(40, DIMS + 1), ALU.mult))
                n.link(nc.vector.tensor_tensor(heads(xl), heads(xl), per_head(44, DIMS + 1), ALU.mult))
                n.link(nc.vector.tensor_tensor(a4, a4, heads(xl), ALU.add))
                n.link(nc.vector.tensor_scalar(small[:, 48:52], a4[:, :, DIMS:DIMS + 1].rearrange("p h d -> p (h d)"),
                                               1.0e-16, None, ALU.add))
                n.link(nc.vector.reciprocal(small[:, 52:56], small[:, 48:52]))
                n.link(nc.vector.tensor_tensor(heads(s), a4[:, :, 0:DIMS], per_head(52, DIMS), ALU.mult))
                nc.vector.tensor_tensor(s, s, bias_sb[:, :], ALU.add).then_inc(neg_out, 1)
                e = nx[:, o, :]
                v.wait_ge(exp_out, b + 1)
                n.link(nc.vector.tensor_scalar(e, e, 1.0, None, ALU.add))
                n.link(nc.vector.reciprocal(e, e))
                n.link(nc.vector.tensor_tensor(s, s, e, ALU.mult))
                nc.vector.tensor_tensor(s, s, xh, ALU.add).then_inc(x1_ready, 1)
                v.wait_ge(x1_ready, b + 1)
                n.link(nc.vector.bn_stats(stats[:, :], s))
                settle(v, s_settled)
                n.link(nc.vector.bn_aggr(mv[:, :], stats[:, :]))
                nc.vector.tensor_scalar(rstd[:, 0:1], mv[:, 1:2], EPS, None, ALU.add).then_inc(rstd_in, 1)
                v.wait_ge(rstd_out, b + (BLOCKS + 1))
                nc.vector.tensor_scalar(e, s, mv[:, 0:1], rstd[:, 1:2], ALU.subtract, ALU.mult).then_inc(z_ready, 1)
                v.wait_ge(z_ready, b + 1)
                v.wait_ge(z_psum, b + 1)
                v.sem_inc(fin_free, 1)
                assert not isinstance(k, int) or n.value == n0 + LINKS
            n.add(nc.vector.memset(small[:, :], 0.0))
            n.wait()
            base[0] = n.value
            v.sem_inc(fin_free, 2)
            run_blocks(v, body)
            n.value = base[0] + BLOCKS * LINKS
            v.wait_ge(zg_copied, BLOCKS)
            v.wait_ge(z_copied, 2 * BLOCKS)
            for o in range(2):
                v.wait_ge(x1_stored[o], 16 * (BLOCKS // 2))
            used[0] = 0
            t = wide_part(BLOCKS, GAT)
            z4 = zg.rearrange("p b (h e) -> p b h e", h=HEADS)
            g4 = gate_rows[:, :, 0:G2.sums].rearrange("p b (h d) -> p b h d", h=HEADS)
            n.link(nc.vector.memset(gate_rows[:, :, :], 1.0))
            for h in range(HEADS):
                n.add(nc.vector.tensor_copy(g4[:, :, h, 0:EXPERTS], z4[:, :, h, :]))
            for c, to in ((0, gate_rows[:, :, G2.sums:G2.width]), (1, adst)):
                n.link(nc.vector.tensor_tensor(t, zg, gat_consts[:, c, :].unsqueeze(1).broadcast_to([P, BLOCKS, GAT]),
                                               ALU.mult))
                n.link(nc.vector.tensor_reduce(to, t.rearrange("p b (h e) -> p b h e", h=HEADS), AX.X, ALU.add))
            n.link(nc.vector.memset(acc2[:, :, :], 0.0))
            nc.vector.memset(max2[:, :, :], NEG).then_inc(gate_rows_ready, 1)
            v.wait_ge(gate_rows_ready, 1)
            v.wait_ge(gate_rows_stored, GATE_STORES)

        gate_exp_in, gate_exp_out = sem("gate_exp_in"), sem("gate_exp_out")
        gates_ready = sem("gates_ready")
        gates = sb("gates", [P, BLOCKS, EXPERTS])
        used[0] = 0
        q_score = wide_part(BLOCKS, HEADS)
        q_max = wide_part(BLOCKS, HEADS)
        q_fall = wide_part(2, BLOCKS, HEADS)
        q_rows = wide_part(BLOCKS, G2.sums)
        q_agg = wide_part(BLOCKS, GAT)
        q_sq = wide_part(BLOCKS, GAT)
        q_mean = wide_part(BLOCKS)
        q_var = wide_part(BLOCKS)
        q_rank = wide_part(BLOCKS, EXPERTS)
        q_cmp = wide_part(BLOCKS)

        def vector_gates(v, n):
            def b3(a, w):
                return a.unsqueeze(2).broadcast_to([P, BLOCKS, w])
            link = n.link
            link(nc.vector.tensor_tensor(q_score, gate_rows[:, :, G2.sums:G2.width], adst, ALU.add))
            link(nc.vector.scalar_tensor_tensor(q_score, q_score, SLOPE, q_score, ALU.mult, ALU.max))
            link(nc.vector.tensor_tensor(q_max, max2[:, :, :], q_score, ALU.max))
            n.add(nc.vector.tensor_tensor(q_fall[:, 0], max2[:, :, :], q_max, ALU.subtract))
            nc.vector.tensor_tensor(q_fall[:, 1], q_score, q_max, ALU.subtract).then_inc(gate_exp_in, 1)
            v.wait_ge(gate_exp_out, 1)
            acc = acc2[:, :, :].rearrange("p b (h d) -> p b h d", h=HEADS)
            rows = gate_rows[:, :, 0:G2.sums].rearrange("p b (h d) -> p b h d", h=HEADS)
            qr = q_rows.rearrange("p b (h d) -> p b h d", h=HEADS)
            wide5 = [P, BLOCKS, HEADS, EXPERTS + 1]
            n.add(nc.vector.tensor_tensor(acc, acc, q_fall[:, 0].unsqueeze(3).broadcast_to(wide5), ALU.mult))
            link(nc.vector.tensor_tensor(qr, rows, q_fall[:, 1].unsqueeze(3).broadcast_to(wide5), ALU.mult))
            link(nc.vector.tensor_tensor(acc2[:, :, :], acc2[:, :, :], q_rows, ALU.add))
            link(nc.vector.tensor_scalar(q_score, acc[:, :, :, EXPERTS], 1.0e-16, None, ALU.add))
            link(nc.vector.reciprocal(q_max, q_score))
            agg = q_agg.rearrange("p b (h d) -> p b h d", h=HEADS)
            link(nc.vector.tensor_tensor(agg, acc[:, :, :, 0:EXPERTS],
                                         q_max.unsqueeze(3).broadcast_to([P, BLOCKS, HEADS, EXPERTS]), ALU.mult))

            def const(c):
                return gat_consts[:, c, :].unsqueeze(1).broadcast_to([P, BLOCKS, GAT])
            link(nc.vector.tensor_tensor(q_agg, q_agg, const(2), ALU.add))
            link(nc.vector.tensor_reduce(q_mean, q_agg, AX.X, ALU.add))
            link(nc.vector.tensor_scalar(q_mean, q_mean, 1.0 / GAT, None, ALU.mult))
            link(nc.vector.tensor_tensor(q_agg, q_agg, b3(q_mean, GAT), ALU.subtract))
            link(nc.vector.tensor_tensor(q_sq, q_agg, q_agg, ALU.mult))
            link(nc.vector.tensor_reduce(q_var, q_sq, AX.X, ALU.add))
            nc.vector.tensor_scalar(q_mean, q_var, 1.0 / GAT, EPS, ALU.mult, ALU.add).then_inc(rstd_in, 1)
            v.wait_ge(rstd_out, 2 * BLOCKS + 1)
            link(nc.vector.tensor_tensor(q_agg, q_agg, b3(q_var, GAT), ALU.mult))
            link(nc.vector.tensor_tensor(q_agg, q_agg, const(3), ALU.mult))
            link(nc.vector.tensor_tensor(q_agg, q_agg, const(4), ALU.add))
            link(nc.vector.tensor_reduce(q_score, q_agg.rearrange("p b (h e) -> p b e h", h=HEADS), AX.X, ALU.add))
            link(nc.vector.tensor_scalar(q_score, q_score, 1.0 / HEADS, None, ALU.mult))
            link(nc.vector.memset(q_rank, 0.0))
            for i in range(EXPERTS):
                for j in range(i + 1, EXPERTS):
                    link(nc.vector.tensor_tensor(q_cmp, q_score[:, :, j], q_score[:, :, i], ALU.is_gt))
                    link(nc.vector.tensor_tensor(q_rank[:, :, i], q_rank[:, :, i], q_cmp, ALU.add))
                    link(nc.vector.tensor_tensor(q_cmp, q_score[:, :, i], q_score[:, :, j], ALU.is_ge))
                    link(nc.vector.tensor_tensor(q_rank[:, :, j], q_rank[:, :, j], q_cmp, ALU.add))
            link(nc.vector.tensor_reduce(q_mean, q_score, AX.X, ALU.max))
            nc.vector.tensor_tensor(q_score, q_score, b3(q_mean, EXPERTS), ALU.subtract).then_inc(gate_exp_in, 1)
            v.wait_ge(gate_exp_out, 2)
            link(nc.vector.scalar_tensor_tensor(q_score, q_rank, 2.0, q_max, ALU.is_lt, ALU.mult))
            link(nc.vector.tensor_reduce(q_mean, q_score, AX.X, ALU.add))
            link(nc.vector.reciprocal(q_var, q_mean))
            nc.vector.tensor_tensor(gates[:, :, :], q_score, b3(q_var, EXPERTS), ALU.mult).then_inc(gates_ready, 1)
            v.wait_ge(gates_ready, 1)

        def scalar_gates(act):
            act.wait_ge(gate_exp_in, 1)
            nc.scalar.activation(q_fall, q_fall, ACT.Exp).then_inc(gate_exp_out, 1)
            act.wait_ge(gate_exp_in, 2)
            nc.scalar.activation(q_max, q_score, ACT.Exp).then_inc(gate_exp_out, 1)

        used[0] = 0
        w1_sb = wide_part(EXPERTS, 2, HIDDEN)
        w2_sb = wide_part(EXPERTS, 4, FEAT)
        hid = wide_part(2, 4, 2 * P)
        b1_sb = sb("b1_sb", [P, EXPERTS, 4])
        b2_sb = sb("b2_sb", [EXPERTS, FEAT])
        x1_t = staged_attr[:, :, :].rearrange("p o n -> p (o n)")[:, 0:4 * FEAT].rearrange(
            "p (o t f) -> p o t f", o=2, t=2)
        out_t = staged_rec[:, :, :].rearrange("p o n -> p (o n)")[:, 0:4 * FEAT].bitcast(F32).rearrange(
            "p (o t f) -> p o t f", o=2, t=2)
        gate_t = sb("gate_t", [P, 2, 2, EXPERTS])
        gateT = attrT[:, :, :].rearrange("p o n -> p (o n)")[0:EXPERTS, 0:2 * P]
        PAIRS = BLOCKS // 2
        w_loaded = sem("expert_weights_loaded")
        EXPERT_WEIGHTS = 64
        x1_loaded = [sem("x1_loaded_a"), sem("x1_loaded_b")]
        gate_copied, gateT_psum, gateT_ready = sem("gate_copied"), sem("gateT_in_psum"), sem("gateT_ready")
        b2_psum, started = sem("b2_in_psum"), sem("output_started")
        hid_psum, hid_ready = sem("hidden_in_psum"), sem("hidden_ready")
        y_psum, y_added = sem("expert_in_psum"), sem("expert_added")
        stored = [sem("stored_a"), sem("stored_b")]

        def run_pairs(engine, body):
            with engine.Fori(0, PAIRS // 2) as k:
                body(k, 0, P)
                body(k, 1, P)
            body(PAIRS // 2, 0, LAST_ROWS)

        def sync_experts(sp):
            sp.wait_ge(gates_ready, 1)
            sp.dma_start(w1_sb, w1.rearrange("e (k p) n -> p e k n", p=P)).then_inc(w_loaded, 16)
            sp.dma_start(w2_sb, w2.rearrange("e (c p) n -> p e c n", p=P)).then_inc(w_loaded, 16)
            sp.dma_start(b1_sb[:, :, :], b1.rearrange("p (e c) -> p e c", e=EXPERTS)).then_inc(w_loaded, 16)
            sp.dma_start(b2_sb[:, :], b2).then_inc(w_loaded, 16)

            def body(k, o, rows):
                q = k * 2 + o
                sp.wait_ge(started, q + 1)
                sp.dma_start(x1_t[:, o, :, :], x1_table[bass.ds(q * (2 * P), 2 * P), :].rearrange(
                    "(t p) f -> p t f", p=P)).then_inc(x1_loaded[o], 16)
            run_pairs(sp, body)

        def scalar_experts(act):
            act.wait_ge(w_loaded, EXPERT_WEIGHTS)

            def body(k, o, rows):
                q = k * 2 + o
                act.wait_ge(gateT_psum, q + 1)
                nc.scalar.copy(gateT, banks[7][0:EXPERTS, 0:2 * P]).then_inc(gateT_ready, 1)
                for e in range(EXPERTS):
                    act.wait_ge(y_psum, q * EXPERTS + (e + 1))
                    for c in range(4):
                        act.wait_ge(hid_psum, q * 16 + (e * 4 + c + 1))
                        nc.scalar.activation(hid[:, e % 2, c, :], banks[c][:, 0:2 * P], ACT.Gelu,
                                             bias=b1_sb[:, e, c:c + 1]).then_inc(hid_ready, 1)
            run_pairs(act, body)

        def tensor_experts(pe):
            pe.wait_ge(w_loaded, EXPERT_WEIGHTS)
            pe.sem_inc(y_psum, 2)

            def body(k, o, rows):
                q = k * 2 + o
                pe.wait_ge(gate_copied, q + 1)
                for t in range(2):
                    last = nc.tensor.transpose(banks[7][0:EXPERTS, t * P:(t + 1) * P], gate_t[:, o, t, :], ident[:, :])
                last.then_inc(gateT_psum, 1)
                z = zT[:, bass.ds(q * 2, 2), :]

                def hidden(e):
                    for c in range(4):
                        i = e * 4 + c
                        pe.wait_ge(hid_ready, q * 16 + (i + 1))
                        for r in range(2):
                            last = nc.tensor.matmul(banks[c][:, 0:2 * P].rearrange("p (t n) -> p t n", t=2),
                                                    w1_sb[:, e, r, c * P:(c + 1) * P], z[:, :, r * P:(r + 1) * P],
                                                    start=(r == 0), stop=(r == 1))
                        last.then_inc(hid_psum, 1)

                def output(e):
                    pe.wait_ge(hid_ready, q * 16 + (e * 4 + 4 + 4))
                    pe.wait_ge(y_added, q * EXPERTS + (e + 1))
                    for t in range(2):
                        for c in range(4):
                            last = nc.tensor.matmul(banks[4 + e % 2][:, t * FEAT:(t + 1) * FEAT],
                                                    hid[:, e % 2, c, t * P:(t + 1) * P], w2_sb[:, e, c, :],
                                                    start=(c == 0), stop=(c == 3))
                    last.then_inc(y_psum, 1)
                hidden(0)
                pe.wait_ge(gateT_ready, q + 1)
                pe.wait_ge(started, q + 2)
                for t in range(2):
                    last = nc.tensor.matmul(banks[6][:, t * FEAT:(t + 1) * FEAT], gateT[:, t * P:(t + 1) * P],
                                            b2_sb[:, :], start=True, stop=True)
                last.then_inc(b2_psum, 1)
                hidden(1)
                output(0)
                hidden(2)
                output(1)
                hidden(3)
                output(2)
                output(3)
            run_pairs(pe, body)

        def vector_experts(v, n):
            v.sem_inc(started, 2)
            v.sem_inc(y_added, 2)
            v.sem_inc(hid_ready, 4)

            def body(k, o, rows):
                q = k * 2 + o
                g2 = gates[:, bass.ds(q * 2, 2), :]
                v.wait_ge(stored[o], k * 32)
                nc.vector.tensor_copy(gate_t[:, o, :, :], g2).then_inc(gate_copied, 1)
                v.wait_ge(x1_loaded[o], k * 16 + 16)
                v.wait_ge(b2_psum, q + 1)
                nc.vector.tensor_tensor(out_t[:, o, :, :], banks[6][:, :].rearrange("p (t f) -> p t f", t=2),
                                        x1_t[:, o, :, :], ALU.add).then_inc(started, 1)
                v.wait_ge(started, q + 3)
                for e in range(EXPERTS):
                    v.wait_ge(y_psum, q * EXPERTS + (e + 3))
                    for t in range(2):
                        last = nc.vector.scalar_tensor_tensor(
                            out_t[:, o, t, :], banks[4 + e % 2][:, t * FEAT:(t + 1) * FEAT],
                            gate_t[:, o, t, e:e + 1], out_t[:, o, t, :], ALU.mult, ALU.add)
                    last.then_inc(y_added, 1)
                    v.wait_ge(y_added, q * EXPERTS + (e + 3))
            run_pairs(v, body)

        def pool_store(pool):
            def body(k, o, rows):
                q = k * 2 + o
                pool.wait_ge(y_added, q * EXPERTS + (EXPERTS + 2))
                for t in range(2):
                    r = rows if t else P
                    pool.dma_start(out[bass.ds(q * (2 * P) + t * P, r), :], out_t[0:r, o, t, :]).then_inc(stored[o], 16)
            run_pairs(pool, body)
            pool.wait_ge(stored[0], 32 * (PAIRS // 2 + 1))
            pool.wait_ge(stored[1], 32 * (PAIRS // 2))

        sig[G1] = Signals(G1)
        sig[G2] = Signals(G2)
        cleared = sem("sums_cleared")
        zero_rows_stored = sem("zero_rows_stored")

        @block.gpsimd
        def _(pool):
            n = pool_constants(pool)
            pool_fill(pool, n)
            done = pool_scatter(pool, G1, 0, n)
            pool_scatter(pool, G2, done, n)
            pool_rstd(pool, BLOCKS)
            for o in range(2):
                pool.wait_ge(node_stored[o], NODE_STORES)
            pool.wait_ge(zero_rows_stored, 32)
            pool_edges_loop(pool, G1)
            pool_rstd(pool, BLOCKS, BLOCKS)
            pool.wait_ge(gate_rows_stored, GATE_STORES)
            pool_edges_loop(pool, G2)
            pool.wait_ge(rstd_in, 2 * BLOCKS + 1)
            nc.gpsimd.tensor_tensor(q_var, q_mean, neg_half[:, :], ALU.pow).then_inc(rstd_out, 1)
            pool_store(pool)

        @block.sync
        def _(sp):
            sync_edges(sp, G1, src1, dst1)
            sync_edges(sp, G2, src2, dst2)
            sync_weights(sp)
            sync_fill(sp)
            sp.wait_ge(s_const, CONSTS)
            sp.dma_start(xl_table[ZERO_ROW:ZERO_ROW + 1, :], zero_row).then_inc(zero_rows_stored, 16)
            sp.dma_start(gate_table[ZERO_ROW:ZERO_ROW + 1, :], zero_row[:, 0:G2.width]).then_inc(zero_rows_stored, 16)
            sync_attr(sp, 0)
            sync_nodes(sp)
            sp.wait_ge(all_scattered[G1], 1)
            sp.wait_ge(blocks_ready[G1], 4)
            for o in range(2):
                sp.wait_ge(node_stored[o], NODE_STORES)
            sync_edges_loop(sp, G1)
            sync_finish(sp)
            sp.wait_ge(all_scattered[G2], 1)
            sp.wait_ge(blocks_ready[G2], 3)
            sp.wait_ge(gate_rows_stored, GATE_STORES)
            sync_edges_loop(sp, G2)
            sync_experts(sp)

        @block.scalar
        def _(act):
            scalar_nodes(act, None)
            for o in range(2):
                act.wait_ge(node_stored[o], NODE_STORES)
            scalar_edges_loop(act, G1)
            scalar_finish(act)
            scalar_edges_loop(act, G2)
            scalar_gates(act)
            scalar_experts(act)

        @block.vector
        def _(v):
            n = Count(v, s_dve)
            nc.vector.memset(ones[:, :], 1.0).then_inc(s_const, 1)
            nc.vector.memset(we_sb[:, :, :], 0.0).then_inc(s_const, 1)
            v.wait_ge(s_const, 6)
            nc.vector.tensor_copy(ident_b[:, :], ident[:, :]).then_inc(s_const, 1)
            nc.vector.memset(zero_row, 0.0).then_inc(s_const, 1)
            vector_buckets(v, G1, n, True)
            vector_buckets(v, G2, n, False)
            vector_nodes(v, n)
            v.wait_ge(all_scattered[G1], 1)
            v.wait_ge(all_scattered[G2], 1)
            v.wait_ge(zero_rows_stored, 32)
            nc.vector.memset(arena[:, :], 0.0).then_inc(cleared, 1)
            nc.vector.memset(max1[:, :, :], NEG).then_inc(cleared, 1)
            v.wait_ge(cleared, 2)
            for o in range(2):
                v.wait_ge(node_stored[o], NODE_STORES)
            vector_edges_loop(v, G1, n)
            vector_finish(v, n)
            vector_edges_loop(v, G2, n)
            vector_gates(v, n)
            vector_experts(v, n)

        @block.tensor
        def _(pe):
            pe.wait_ge(s_const, CONSTS)
            tensor_buckets(pe, G1, 0)
            tensor_buckets(pe, G2, 1)
            tensor_nodes(pe)
            tensor_edges_loop(pe, G1)
            tensor_finish(pe)
            tensor_edges_loop(pe, G2)
            tensor_experts(pe)


def kernel(x, src, dst, edge_attr_16, L0_gnn_W_l, L0_gnn_b_l, L0_gnn_W_r, L0_gnn_b_r, L0_gnn_W_e,
           L0_gnn_att, L0_gnn_bias, L0_ffn_W_gat, L0_ffn_att_src, L0_ffn_att_dst, L0_ffn_b_gat,
           L0_ffn_ln_gamma, L0_ffn_ln_beta, L0_ffn_W1, L0_ffn_b1, L0_ffn_W2, L0_ffn_b2,
           L0_ffn_edge_index):
    import numpy as np
    import concourse.bacc as bacc
    from concourse.bass_utils import run_bass_kernel_spmd

    def lay(a):
        return np.ascontiguousarray(np.asarray(a))

    arrays = {
        "x": lay(x), "src1": lay(src), "dst1": lay(dst), "attr": lay(edge_attr_16),
        "w_lr": lay(np.concatenate([np.asarray(L0_gnn_W_l).T, np.asarray(L0_gnn_W_r).T], axis=1)),
        "b_lr": lay(np.concatenate([np.asarray(L0_gnn_b_l), np.asarray(L0_gnn_b_r)])[None, :]),
        "w_e": lay(np.asarray(L0_gnn_W_e).T), "att": lay(np.asarray(L0_gnn_att).reshape(-1)),
        "bias": lay(L0_gnn_bias), "w_gat": lay(L0_ffn_W_gat),
        "att_src": lay(np.asarray(L0_ffn_att_src).reshape(-1)),
        "att_dst": lay(np.asarray(L0_ffn_att_dst).reshape(-1)), "b_gat": lay(L0_ffn_b_gat),
        "ln_gamma": lay(L0_ffn_ln_gamma), "ln_beta": lay(L0_ffn_ln_beta),
        "w1": lay(L0_ffn_W1), "b1": lay(np.asarray(L0_ffn_b1).reshape(EXPERTS * 4, P).T), "w2": lay(L0_ffn_W2), "b2": lay(L0_ffn_b2),
        "src2": lay(np.asarray(L0_ffn_edge_index)[0]), "dst2": lay(np.asarray(L0_ffn_edge_index)[1]),
    }
    nc = bacc.Bacc("TRN2", target_bir_lowering=False, num_devices=1)
    args = {name: nc.dram_tensor(name, a.shape, mybir.dt.from_np(a.dtype), kind="ExternalInput").ap()
            for name, a in arrays.items()}
    args["out"] = nc.dram_tensor("out", [NODES, FEAT], F32, kind="ExternalOutput").ap()
    build(nc, **args)
    result = run_bass_kernel_spmd(nc, [arrays], core_ids=[0])
    return result.results[0]["out"]
```

```python
from contextlib import ExitStack

import concourse.bass as bass
from concourse import mybir

F32 = mybir.dt.float32
BF16 = mybir.dt.bfloat16
I32 = mybir.dt.int32
ALU = mybir.AluOpType
ACT = mybir.ActivationFunctionType
AX = mybir.AxisListType

P = 128
NODES, FEAT, HEADS, EDGE_DIM = 12500, 256, 4, 16
DIMS = FEAT // HEADS
BLOCKS = -(-NODES // P)
LAST_ROWS = NODES - (BLOCKS - 1) * P
NODES_PAD = BLOCKS * P
ZERO_ROW = NODES_PAD
EXPERTS, HIDDEN = 4, 512
GAT = HEADS * EXPERTS
NEG = -1.0e30
GROUP = 4
SLOTS = 4
UNROLL = 8
SLOPE = 0.2
EPS = 1.0e-5


class Graph:

    def __init__(self, name, edges, rows, chunk, dims, width, words, extra):
        self.name, self.edges, self.rows, self.cols, self.chunk = name, edges, rows, edges // rows, chunk
        self.dims, self.width, self.words, self.extra = dims, width, words, extra
        self.sums = HEADS * (dims + 1)
        self.acc = self.sums + extra
        tiles = (edges + BLOCKS * (P - 1)) // P
        self.groups = -(-tiles // GROUP)
        self.tiles = self.groups * GROUP
        assert self.rows * self.cols == edges and self.cols % (2 * chunk) == 0


G1 = Graph("gnn", 200000, 125, 32, DIMS, HEADS * (DIMS + 1), 2 + EDGE_DIM + 1, EDGE_DIM + 1)
G2 = Graph("ffn", 131072, 128, 32, EXPERTS, HEADS * (EXPERTS + 1) + HEADS, 2, 0)


class Count:

    def __init__(self, engine, semaphore):
        self.engine, self.semaphore, self.value = engine, semaphore, 0

    def add(self, instruction):
        instruction.then_inc(self.semaphore, 1)
        self.value = self.value + 1

    def wait(self):
        self.engine.wait_ge(self.semaphore, self.value)

    def link(self, instruction):
        self.add(instruction)
        self.wait()


def settle(engine, s_settled):
    engine.sem_inc(s_settled, 1)


class Step:

    def __init__(self, k, o):
        self.k, self.o = k, o
        self.g = k * UNROLL + o
        self.slot = o % SLOTS
        self.uses = k * (UNROLL // SLOTS) + o // SLOTS
        self.half = o % 2
        self.half_uses = k * (UNROLL // 2) + o // 2
        self.rec = o % UNROLL
        self.rec_uses = k + o // UNROLL

    def near(self, d):
        return Step(self.k, self.o + d)


def step_of(g):
    return Step(g // UNROLL, g % UNROLL)


def wait(engine, semaphore, value):
    if not (isinstance(value, int) and value <= 0):
        engine.wait_ge(semaphore, value)


def run_all(engine, groups, body, between=None, between_runs=0):
    for g in range(UNROLL):
        body(step_of(g))
    runs = groups // UNROLL - 1
    if between_runs:
        with engine.Fori(1, 1 + between_runs) as k:
            for o in range(UNROLL):
                body(Step(k, o))
                between(k, o)
    with engine.Fori(1 + between_runs, 1 + runs) as k:
        for o in range(UNROLL):
            body(Step(k, o))
    for g in range(UNROLL * (1 + runs), groups):
        body(step_of(g))


AHEAD = 3


def run_groups(engine, groups, body):
    for g in range(UNROLL):
        body(step_of(g), groups - 1 - g)
    runs = (groups - AHEAD - UNROLL) // UNROLL
    with engine.Fori(1, 1 + runs) as k:
        for o in range(UNROLL):
            body(Step(k, o), AHEAD)
    for g in range(UNROLL * (1 + runs), groups):
        body(step_of(g), groups - 1 - g)


def build(nc, x, src1, dst1, attr, w_lr, b_lr, w_e, att, bias, w_gat, att_src, att_dst, b_gat,
          ln_gamma, ln_beta, w1, b1, w2, b2, src2, dst2, out):
    ctx = ExitStack()
    with ctx:
        def sb(name, shape, dt=F32):
            return ctx.enter_context(nc.sbuf_tensor(name, shape, dt))

        def pb(name, shape, dt=F32):
            return ctx.enter_context(nc.psum_tensor(name, shape, dt))

        def sem(name):
            return ctx.enter_context(nc.semaphore(name))

        def dram(name, shape, dt=F32):
            return nc.dram_tensor(name, shape, dt, kind="Internal").ap()

        xl_table = dram("xl_table", [NODES_PAD + 1, G1.width])
        xr_table = dram("xr_table", [NODES_PAD, FEAT])
        xh_table = dram("xh_table", [NODES_PAD, FEAT])
        x1_table = dram("x1_table", [NODES_PAD, FEAT])
        gate_table = dram("gate_table", [NODES_PAD + 1, G2.width])
        adst_table = dram("adst_table", [NODES_PAD, HEADS])
        records = {G1: dram("records1", [P, G1.tiles * G1.words], I32),
                   G2: dram("records2", [P, G2.tiles * G2.words], I32)}
        gathered = {G1: xl_table, G2: gate_table}
        targets = {G1: (xr_table, FEAT), G2: (adst_table, HEADS)}

        arena = sb("arena", [P, BLOCKS * G1.acc])
        acc1 = arena[:, :].rearrange("p (b n) -> p b n", n=G1.acc)
        zT = acc1[:, :, 0:FEAT]
        acc2 = sb("acc2", [P, BLOCKS, G2.acc])
        max1 = sb("max1", [P, BLOCKS, HEADS])
        max2 = sb("max2", [P, BLOCKS, HEADS])
        accs, maxs = {G1: acc1, G2: acc2[:, :, :]}, {G1: max1, G2: max2}
        gate_rows = sb("gate_rows", [P, BLOCKS, G2.width])
        gate_flat = gate_rows[:, :, :].rearrange("p b n -> p (b n)")
        block_of = {G1: gate_flat[0:1, 0:G1.tiles].bitcast(I32), G2: sb("block_of2", [1, G2.tiles], I32)}

        ident = sb("ident", [P, P])
        ident_b = sb("ident_b", [P, P], BF16)
        before = sb("before", [P, P])
        ones = sb("ones", [P, P])
        iota = sb("iota", [P, P])
        wlr_sb = sb("wlr_sb", [P, 2, 2 * FEAT])
        blr_sb = sb("blr_sb", [1, 2 * FEAT])
        we_sb = sb("we_sb", [GROUP * G1.words, GROUP, FEAT])
        att_sb = sb("att_sb", [P, FEAT])
        bias_sb = sb("bias_sb", [P, FEAT])
        wgat_sb = sb("wgat_sb", [P, 2, GAT])
        gat_consts = sb("gat_consts", [P, 5, GAT])
        neg_half = sb("neg_half", [P, BLOCKS])

        at = [0]

        def part(width, dt=F32):
            lo = at[0]
            at[0] = lo + width
            assert at[0] <= BLOCKS * G1.acc
            a = arena[:, lo:lo + width]
            return a if dt == F32 else a.bitcast(dt)

        bucket = {}
        for g in (G1, G2):
            b = bucket[g] = {}
            for n, dt in (("dst", I32), ("src", I32), ("block", F32), ("within", F32)):
                b[n] = part(g.cols, dt)
            b["slot"] = b["dst"]
            b["rank"] = part(g.cols)
        hit, hits_so_far, picked = part(G1.cols), part(G1.tiles), part(G1.cols)
        hit_i, tile_i = hit.bitcast(I32), picked.bitcast(I32)
        passed = hits_so_far
        tile_iota_store = part(G1.tiles)
        counts = part(BLOCKS)
        tiles_of = part(BLOCKS)
        tiles_i = part(BLOCKS, I32)
        tile_end = part(BLOCKS)
        first_slot = part(BLOCKS)
        end_col = part(1)
        held_slot = acc2[:, :, :].rearrange("p b n -> p (b n)")[:, 0:G2.cols].bitcast(I32)
        held_within = gate_flat[:, G1.tiles:G1.tiles + G2.cols // 2].bitcast(BF16)
        staged_slot = sb("staged_slot", [P, 2, G1.chunk], I32)
        staged_rec = sb("staged_rec", [P, 2, G1.chunk * G1.words], I32)
        rec_flat = staged_rec[:, :, :].rearrange("p o n -> p (o n)")
        held_src = rec_flat[:, 0:G2.cols]
        staged_rec2 = rec_flat[:, G2.cols:G2.cols + G2.chunk * G2.words]
        staged_attr = sb("staged_attr", [P, 2, G1.chunk * EDGE_DIM])

        rec = sb("rec", [P, UNROLL, GROUP * G1.words], I32)
        WIDE = 10304
        wide = sb("wide", [P, WIDE])
        used = [0]

        def wide_part(*shape):
            size = 1
            for d in shape:
                size *= d
            lo = used[0]
            used[0] = lo + size
            assert used[0] <= WIDE
            names = " ".join(f"d{i}" for i in range(len(shape)))
            return wide[:, lo:lo + size].rearrange(f"p ({names}) -> p {names}",
                                                   **{f"d{i}": d for i, d in enumerate(shape)})

        tab = wide_part(SLOTS, GROUP * G1.width)
        trow = wide_part(2, GROUP * FEAT)
        oh = wide_part(SLOTS, GROUP, P)
        ohT = wide_part(SLOTS, GROUP, P)
        pen = sb("pen", [P, SLOTS, GROUP * P], BF16)
        attrT = sb("attrT", [GROUP * G1.words, SLOTS, P])
        relu = staged_attr[:, :, :].rearrange("p o n -> p (o n)")[:, 0:GROUP * FEAT]
        score = sb("score", [P, SLOTS, GROUP * HEADS])
        score_hi = sb("score_hi", [P, 2, GROUP * HEADS], BF16)
        score_lo = sb("score_lo", [P, 2, GROUP * HEADS], BF16)
        tmax = sb("tmax", [P, GROUP, HEADS])
        old_max = sb("old_max", [P, GROUP, HEADS])
        new_max = sb("new_max", [P, SLOTS, GROUP * HEADS])
        fall = sb("fall", [P, SLOTS, GROUP * HEADS])
        rescale = sb("rescale", [P, SLOTS, GROUP * HEADS])
        shifted = sb("shifted", [P, GROUP * HEADS])
        weight = sb("weight", [P, GROUP * HEADS])

        used[0] = 0
        nx = wide_part(2, 2, FEAT)
        nh = wide_part(2, 2, FEAT)
        nxh = wide_part(2, 2, FEAT)
        nhT = wide_part(2, 2, FEAT)
        nxl = wide_part(2, 2, HEADS * (DIMS + 1))
        nxr = wide_part(2, 2, FEAT)
        stats = sb("stats", [P, 2, 6])
        mv = sb("mv", [P, 2, 2, 2])
        variance = sb("variance", [P, 2, 2])
        root = sb("root", [P, 2])
        rstd = sb("rstd", [P, 2, 2])
        small = sb("small", [P, 2, 56])
        laT = attrT[:, :, :].rearrange("p o n -> p (o n)")[0:2 + EDGE_DIM, 0:2 * P]

        zg = acc1[:, :, FEAT:FEAT + GAT]
        adst = acc1[:, :, FEAT + GAT:FEAT + GAT + HEADS]

        banks = [pb(f"bank{n}", [P, 512]) for n in range(8)]

        s_const = sem("constants_made")
        s_settled = sem("settled")
        s_weights = sem("weights_loaded")
        s_dve = sem("vector_step_done")
        s_pool = sem("pool_step_done")
        edges_loaded = {g: sem(f"edges_loaded_{g.name}") for g in (G1, G2)}
        s_bucket_mm = sem("bucket_product_done")
        s_bucket_in = sem("bucket_operand_ready")
        slots_ready = {g: sem(f"slots_ready_{g.name}") for g in (G1, G2)}
        blocks_ready = {g: sem(f"blocks_ready_{g.name}") for g in (G1, G2)}
        filler_made = sem("filler_made")
        filled = sem("records_filled")
        scattered = [sem("scattered_a"), sem("scattered_b")]
        all_scattered = {G1: sem("all_scattered_gnn")}
        scattered2, staged2 = sem("scattered_ffn"), sem("staged_ffn")
        held = sem("slots_held")
        attr_loaded = [sem("attr_loaded_a"), sem("attr_loaded_b")]
        attr_used = sem("attr_used")

        block = ctx.enter_context(nc.Block())

        def pool_constants(pool):
            n = Count(pool, s_pool)
            n.add(nc.gpsimd.memset(ident[:, :], 0.0))
            n.add(nc.gpsimd.memset(before[:, :], 1.0))
            n.link(nc.gpsimd.memset(neg_half[:, :], -0.5))
            nc.gpsimd.affine_select(out=ident[:, :], in_=ident[:, :], compare_op=ALU.not_equal, fill=1.0,
                                    base=0, pattern=[[-1, P]], channel_multiplier=1).then_inc(s_const, 1)
            nc.gpsimd.affine_select(out=before[:, :], in_=before[:, :], compare_op=ALU.is_gt, fill=0.0,
                                    base=0, pattern=[[1, P]], channel_multiplier=-1).then_inc(s_const, 1)
            nc.gpsimd.iota(iota[:, :], [[1, P]], base=0, channel_multiplier=0,
                           allow_small_or_imprecise_dtypes=True).then_inc(s_const, 1)
            nc.gpsimd.iota(tile_iota_store[:, :], [[1, G1.tiles]], base=0, channel_multiplier=0,
                           allow_small_or_imprecise_dtypes=True).then_inc(s_const, 1)
            return n

        def sync_weights(sp):
            sp.dma_start(wlr_sb[:, :, :], w_lr.rearrange("(k p) n -> p k n", p=P)).then_inc(s_weights, 16)
            sp.dma_start(blr_sb[:, :], b_lr).then_inc(s_weights, 16)
            sp.dma_start(wgat_sb[:, :, :], w_gat.rearrange("(k p) n -> p k n", p=P)).then_inc(s_weights, 16)
            sp.dma_start(att_sb[:, :], att.partition_broadcast(P)).then_inc(s_weights, 16)
            sp.dma_start(bias_sb[:, :], bias.partition_broadcast(P)).then_inc(s_weights, 16)
            for n, v in enumerate((att_src, att_dst, b_gat, ln_gamma, ln_beta)):
                sp.dma_start(gat_consts[:, n, :], v.partition_broadcast(P)).then_inc(s_weights, 16)
            sp.wait_ge(s_const, 6)
            for j in range(GROUP):
                sp.dma_start(we_sb[G1.words * j + 2:G1.words * j + 2 + EDGE_DIM, j, :], w_e).then_inc(s_weights, 16)

        RANK_PARTS = 5
        WEIGHTS = 16 * (10 + GROUP)
        CONSTS = 8

        def sync_edges(sp, g, src, dst):
            b, r = bucket[g], g.rows
            sp.dma_start(b["dst"][0:r, :], dst.rearrange("(p c) -> p c", p=r)).then_inc(edges_loaded[g], 16)
            sp.dma_start(b["src"][0:r, :], src.rearrange("(p c) -> p c", p=r)).then_inc(edges_loaded[g], 16)

        def vector_buckets(v, g, n, first):
            b, r, c = bucket[g], g.rows, g.cols
            v.wait_ge(edges_loaded[g], 32)
            if first:
                v.wait_ge(s_const, CONSTS)
            n.add(nc.vector.tensor_scalar(tile_i[0:r, 0:c], b["dst"][0:r, :], 7, None, ALU.arith_shift_right))
            n.link(nc.vector.tensor_scalar(hit_i[0:r, 0:c], b["dst"][0:r, :], P - 1, None, ALU.bitwise_and))
            n.add(nc.vector.tensor_copy(b["block"][0:r, :], tile_i[0:r, 0:c]))
            n.add(nc.vector.tensor_copy(b["within"][0:r, :], hit_i[0:r, 0:c]))
            n.link(nc.vector.memset(b["rank"][0:r, :], 0.0))
            n0 = n.value
            with v.Fori(0, BLOCKS) as h:
                n.value = n0 + h
                n.link(nc.vector.tensor_scalar(hit[0:r, 0:c], b["block"][0:r, :], iota[0:r, bass.ds(h, 1)],
                                               0.0, ALU.is_equal, ALU.add,
                                               accum_out=counts[0:r, bass.ds(h, 1)]))
            n.value = n0 + BLOCKS
            nc.vector.tensor_copy(counts[0:1, 0:1], counts[0:1, 0:1]).then_inc(s_bucket_in, 1)
            k = 0 if first else 1
            v.wait_ge(s_bucket_mm, 4 * k + 1)
            n.link(nc.vector.tensor_scalar(tiles_i[:, :], banks[0][:, 0:BLOCKS], float(P - 1), None, ALU.add))
            n.link(nc.vector.tensor_scalar(tiles_i[:, :], tiles_i[:, :], 7, None, ALU.arith_shift_right))
            n.link(nc.vector.tensor_copy(tiles_of[:, :], tiles_i[:, :]))
            nc.vector.tensor_tensor_scan(tile_end[:, :], tiles_of[:, :], tiles_of[:, :], 0.0,
                                         ALU.add, ALU.max).then_inc(s_bucket_in, 1)
            v.wait_ge(s_bucket_in, 3 * k + 2)
            n.link(nc.vector.tensor_tensor(first_slot[:, :], tile_end[:, :], tiles_of[:, :], ALU.subtract))
            n.link(nc.vector.scalar_tensor_tensor(first_slot[:, :], first_slot[:, :], float(P),
                                                  banks[1][:, 0:BLOCKS], ALU.mult, ALU.add))
            v.wait_ge(s_bucket_mm, 4 * k + 2)
            n.link(nc.vector.tensor_copy(end_col[0:BLOCKS, :], banks[2][0:BLOCKS, 0:1]))
            nc.vector.tensor_scalar(passed[0:BLOCKS, 0:g.tiles], tile_iota_store[0:BLOCKS, 0:g.tiles],
                                    end_col[0:BLOCKS, 0:1], None, ALU.is_ge).then_inc(s_bucket_in, 1)
            v.wait_ge(s_bucket_mm, 4 * k + 3)
            for m, lo in enumerate(range(0, g.tiles, 512)):
                hi = min(g.tiles, lo + 512)
                nc.vector.tensor_scalar(block_of[g][0:1, lo:hi], banks[4 + m][0:1, 0:hi - lo],
                                        float(BLOCKS - 1), None, ALU.min).then_inc(blocks_ready[g], 1)
            parts = RANK_PARTS if first else 2
            pc = c // parts
            rank_i = b["slot"]
            for q in range(parts):
                cols = slice(q * pc, (q + 1) * pc)
                n0 = n.value
                with v.Fori(0, BLOCKS // 2) as hh:
                    n.value = n0 + hh * 6
                    hits = [hit[0:r, d * pc:(d + 1) * pc] for d in range(2)]
                    sofar = [hits_so_far[0:r, d * pc:(d + 1) * pc] for d in range(2)]
                    carry = [first_slot[0:r, bass.ds(hh * 2 + d, 1)] for d in range(2)]
                    for d in range(2):
                        n.add(nc.vector.tensor_scalar(hits[d], b["block"][0:r, cols],
                                                      iota[0:r, bass.ds(hh * 2 + d, 1)], None, ALU.is_equal))
                    n.wait()
                    for d in range(2):
                        n.add(nc.vector.tensor_tensor_scan(sofar[d], hits[d], hits[d], carry[d], ALU.add, ALU.max))
                    n.wait()
                    settle(v, s_settled)
                    n.link(nc.vector.copy_predicated(b["rank"][0:r, cols], hits[0].bitcast(I32), sofar[0]))
                    for d in range(2):
                        nc.vector.tensor_scalar(carry[d], sofar[d][:, pc - 1:pc], 0.0, None, ALU.add)
                    n.link(nc.vector.copy_predicated(b["rank"][0:r, cols], hits[1].bitcast(I32), sofar[1]))
                n.value = n0 + 3 * BLOCKS
                n.link(nc.vector.tensor_scalar(rank_i[0:r, cols], b["rank"][0:r, cols], -1.0, None, ALU.add))
                n.add(nc.vector.tensor_scalar(tile_i[0:r, 0:pc], rank_i[0:r, cols], 7, None,
                                              ALU.arith_shift_right))
                n.link(nc.vector.tensor_scalar(hit_i[0:r, 0:pc], rank_i[0:r, cols], P - 1, None, ALU.bitwise_and))
                n.link(nc.vector.scalar_tensor_tensor(rank_i[0:r, cols], hit_i[0:r, 0:pc], float(g.tiles),
                                                      tile_i[0:r, 0:pc], ALU.mult, ALU.add))
                if first:
                    v.sem_inc(slots_ready[g], c // (2 * g.chunk) // parts)

        def tensor_buckets(pe, g, k):
            r = g.rows
            pe.wait_ge(s_bucket_in, 3 * k + 1)
            nc.tensor.matmul(banks[0][:, 0:BLOCKS], ones[0:r, :], counts[0:r, :], start=True, stop=True)
            nc.tensor.matmul(banks[1][:, 0:BLOCKS], before[0:r, :], counts[0:r, :],
                             start=True, stop=True).then_inc(s_bucket_mm, 1)
            pe.wait_ge(s_bucket_in, 3 * k + 2)
            nc.tensor.transpose(banks[2][0:BLOCKS, 0:P], tile_end[:, :], ident[:, :]).then_inc(s_bucket_mm, 1)
            pe.wait_ge(s_bucket_in, 3 * k + 3)
            last = None
            for m, lo in enumerate(range(0, g.tiles, 512)):
                hi = min(g.tiles, lo + 512)
                last = nc.tensor.matmul(banks[4 + m][0:1, 0:hi - lo], ones[0:BLOCKS, 0:1],
                                        passed[0:BLOCKS, lo:hi], start=True, stop=True)
            last.then_inc(s_bucket_mm, 2)

        def sync_fill(sp):
            sp.wait_ge(filler_made, 2)
            for g in (G1, G2):
                per = g.tiles // 4 * g.words
                for q in range(4):
                    sp.dma_start(records[g][:, q * per:(q + 1) * per], filler(g)).then_inc(filled, 16)

        def filler(g):
            return fillers[g][:, 0:g.tiles // 4 * g.words]

        fillers = {G1: None, G2: None}
        zero_row = part(G1.width)[0:1, :]
        fillers[G1] = wide[:, 0:G1.tiles // 4 * G1.words].bitcast(I32)
        fillers[G2] = gate_flat[:, G1.tiles:G1.tiles + G2.tiles // 4 * G2.words].bitcast(I32)

        def pool_fill(pool, n):
            for g in (G1, G2):
                n.link(nc.gpsimd.memset(filler(g), 0))
            for g in (G1, G2):
                f = filler(g).rearrange("p (t w) -> p t w", w=g.words)
                n.link(nc.gpsimd.memset(f[:, :, 0:1], ZERO_ROW))
                nc.gpsimd.memset(f[:, :, 1:2].bitcast(F32), -1.0).then_inc(filler_made, 1)

        def pool_scatter1(pool, n):
            g = G1
            b, r, ch, w = bucket[g], g.rows, g.chunk, g.words
            pool.wait_ge(filled, 16 * 8)
            out_rows = records[g].rearrange("p (t w) -> (p t) w", w=w)

            def as3(a):
                return a.rearrange("p (c w) -> p c w", w=1)

            a = attr.rearrange("(p c) d -> p (c d)", p=r)

            def load(k, o):
                pool.dma_start(staged_attr[0:r, o, :],
                               a[:, bass.ds((k * 2 + o) * (ch * EDGE_DIM), ch * EDGE_DIM)]).then_inc(attr_loaded[o], 16)

            def chunk(k, o, more=True):
                c = (k * 2 + o) * ch
                wait(pool, slots_ready[g], k + 1)
                wait(pool, scattered[o], k * (16 * ch))
                settle(pool, s_settled)
                rv = staged_rec[0:r, o, 0:ch * w].rearrange("p (c w) -> p c w", w=w)
                rf = rv.bitcast(F32)
                nc.gpsimd.tensor_copy(staged_slot[0:r, o, 0:ch], b["slot"][0:r, bass.ds(c, ch)])
                nc.gpsimd.tensor_copy(rv[:, :, 0:1], as3(b["src"][0:r, bass.ds(c, ch)]))
                n.link(nc.gpsimd.tensor_copy(rf[:, :, 1:2], as3(b["within"][0:r, bass.ds(c, ch)])))
                settle(pool, s_settled)
                pool.wait_ge(attr_loaded[o], k * 16 + 16)
                settle(pool, s_settled)
                nc.gpsimd.tensor_copy(
                    rf[:, :, 2:2 + EDGE_DIM],
                    staged_attr[0:r, o, :].rearrange("p (c d) -> p c d", d=EDGE_DIM)).then_inc(attr_used, 1)
                pool.wait_ge(attr_used, k * 2 + (o + 1))
                settle(pool, s_settled)
                if more:
                    load(k + 1, o)
                for j in range(ch):
                    nc.gpsimd.indirect_dma_start(
                        out=out_rows, out_offset=bass.IndirectOffsetOnAxis(ap=staged_slot[0:r, o, j:j + 1], axis=0),
                        in_=staged_rec[0:r, o, j * w:(j + 1) * w], in_offset=None).then_inc(scattered[o], 16)

            for o in range(2):
                rv = staged_rec[:, o, :].rearrange("p (c w) -> p c w", w=w)
                n.link(nc.gpsimd.memset(rv[:, :, w - 1:w].bitcast(F32), 1.0))
            load(0, 0)
            load(0, 1)
            chunk(0, 0)
            chunk(0, 1)
            n0 = n.value
            turns = g.cols // (2 * ch)
            with pool.Fori(1, turns - 1) as k:
                n.value = n0 + (k - 1) * 2
                chunk(k, 0)
                chunk(k, 1)
            n.value = n0 + (turns - 2) * 2
            chunk(turns - 1, 0, False)
            chunk(turns - 1, 1, False)
            for o in range(2):
                pool.wait_ge(scattered[o], 16 * (g.cols // 2))
            pool.sem_inc(all_scattered[g], 1)

        SCATTER2_RUNS = G2.cols // G2.chunk

        def pool_scatter2(pool, k, o):
            g = G2
            ch, w = g.chunk, g.words
            if o == 0:
                c = (k - 1) * ch
                wait(pool, scattered2, (k - 1) * (16 * ch))
                settle(pool, s_settled)
                rv = staged_rec2.rearrange("p (c w) -> p c w", w=w)

                def as3(a):
                    return a.rearrange("p (c w) -> p c w", w=1)
                nc.gpsimd.tensor_copy(staged_slot[:, 0, 0:ch], held_slot[:, bass.ds(c, ch)])
                nc.gpsimd.tensor_copy(rv[:, :, 0:1], as3(held_src[:, bass.ds(c, ch)]))
                nc.gpsimd.tensor_copy(rv[:, :, 1:2].bitcast(F32),
                                      as3(held_within[:, bass.ds(c, ch)])).then_inc(staged2, 1)
                wait(pool, staged2, k)
                settle(pool, s_settled)
            out_rows = records[g].rearrange("p (t w) -> (p t) w", w=w)
            for j in range(o * ch // UNROLL, (o + 1) * ch // UNROLL):
                nc.gpsimd.indirect_dma_start(
                    out=out_rows, out_offset=bass.IndirectOffsetOnAxis(ap=staged_slot[:, 0, j:j + 1], axis=0),
                    in_=staged_rec2[:, j * w:(j + 1) * w], in_offset=None).then_inc(scattered2, 16)

        x_loaded = [sem("x_loaded_a"), sem("x_loaded_b")]
        x_last_loaded = sem("x_last_loaded")
        h_ready, xh_ready = sem("h_ready"), sem("xh_ready")
        hT_in_psum, hT_ready = sem("hT_in_psum"), sem("hT_ready")
        lr_in_psum, lr_ready = sem("lr_in_psum"), sem("lr_ready")
        node_stored = [sem("node_stored_a"), sem("node_stored_b")]
        variance_ready, root_ready = sem("node_variance_ready"), sem("node_root_ready")
        rstd_in, rstd_out = sem("variance_ready"), sem("rstd_ready")
        nxl_made = sem("nxl_made")
        PAIRS = BLOCKS // 2

        def run_pairs(engine, body):
            body(0, 0, P)
            body(0, 1, P)
            with engine.Fori(1, PAIRS // 2) as k:
                body(k, 0, P)
                body(k, 1, P)
            body(PAIRS // 2, 0, LAST_ROWS)

        def pair_rows(table, q):
            return table[bass.ds(q * (2 * P), 2 * P), :].rearrange("(t p) f -> p t f", p=P)

        def flat(a):
            return a.rearrange("p t f -> p (t f)")

        def sync_nodes(sp):
            def body(k, o, rows):
                q = k * 2 + o
                wait(sp, xh_ready, q - 1)
                if rows == P:
                    sp.dma_start(nx[:, o, :, :], pair_rows(x, q)).then_inc(x_loaded[o], 16)
                else:
                    sp.dma_start(nx[:, o, 0, :], x[bass.ds(q * (2 * P), P), :]).then_inc(x_last_loaded, 16)
                    sp.wait_ge(x_last_loaded, 16)
                    sp.dma_start(nx[0:rows, o, 1, :], x[bass.ds(q * (2 * P) + P, rows), :]).then_inc(x_loaded[o], 16)
            sp.wait_ge(filled, 16 * 8)
            run_pairs(sp, body)

        def scalar_nodes(act):
            def roots(q):
                wait(act, variance_ready, q + 1)
                nc.scalar.activation(root[:, :], variance[:, 0, :], ACT.Sqrt).then_inc(root_ready, 1)

            def body(k, o, rows):
                q = k * 2 + o
                wait(act, hT_in_psum, q + 1)
                nc.scalar.copy(flat(nhT[:, o, :, :]), banks[o][:, :]).then_inc(hT_ready, 1)
                if rows == P:
                    roots(q + 1)
                wait(act, node_stored[o], k * 48)
                for t in range(2):
                    wait(act, lr_in_psum, q * 2 + (t + 1))
                    bank = banks[2 + 2 * o + t]
                    nc.scalar.copy(nxl[:, o, t, :].rearrange("p (h d) -> p h d", h=HEADS)[:, :, 0:DIMS],
                                   bank[:, 0:FEAT].rearrange("p (h d) -> p h d", h=HEADS)).then_inc(lr_ready, 1)
                    nc.scalar.copy(nxr[:, o, t, :], bank[:, FEAT:2 * FEAT]).then_inc(lr_ready, 1)
                wait(act, lr_ready, q * 4 + 4)
                act.dma_start(pair_rows(xl_table, q), nxl[:, o, :, :]).then_inc(node_stored[o], 16)
                act.dma_start(pair_rows(xr_table, q), nxr[:, o, :, :]).then_inc(node_stored[o], 16)
                wait(act, xh_ready, q + 1)
                act.dma_start(pair_rows(xh_table, q), nxh[:, o, :, :]).then_inc(node_stored[o], 16)
            act.wait_ge(nxl_made, 1)
            roots(0)
            run_pairs(act, body)

        def wait_nodes_stored(engine):
            engine.wait_ge(node_stored[0], 48 * (PAIRS // 2 + 1))
            engine.wait_ge(node_stored[1], 48 * (PAIRS // 2))

        def vector_nodes(v, n):
            v.wait_ge(filled, 16 * 8)
            nc.vector.memset(nxl[:, :, :, :], 1.0).then_inc(nxl_made, 1)
            base = n.value
            LINKS = 5

            def statistics(k, o):
                v.wait_ge(x_loaded[o], k * 16 + 16)
                n.add(nc.vector.bn_stats(stats[:, 0, :], nx[:, o, 0, :]))
                n.link(nc.vector.bn_stats(stats[:, 1, :], nx[:, o, 1, :]))
                settle(v, s_settled)
                n.add(nc.vector.bn_aggr(mv[:, o, 0, :], stats[:, 0, :]))
                n.link(nc.vector.bn_aggr(mv[:, o, 1, :], stats[:, 1, :]))
                nc.vector.tensor_scalar(variance[:, 0, :], mv[:, o, :, 1], EPS, None,
                                        ALU.add).then_inc(variance_ready, 1)

            def body(k, o, rows):
                q = k * 2 + o
                n.value = base + 4 + q * LINKS
                wait(v, root_ready, q + 1)
                n.link(nc.vector.reciprocal(rstd[:, o, :], root[:, :]))
                wait(v, hT_in_psum, q - 1)
                for t in range(2):
                    last = nc.vector.tensor_scalar(nh[:, o, t, :], nx[:, o, t, :], mv[:, o, t, 0:1],
                                                   rstd[:, o, t:t + 1], ALU.subtract, ALU.mult)
                last.then_inc(h_ready, 1)
                if rows == P:
                    statistics(k + o, 1 - o)
                wait(v, h_ready, q + 1)
                wait(v, node_stored[o], k * 48)
                nc.vector.tensor_tensor(flat(nxh[:, o, :, :]), flat(nx[:, o, :, :]), flat(nh[:, o, :, :]),
                                        ALU.add).then_inc(xh_ready, 1)
            n.value = base
            statistics(0, 0)
            run_pairs(v, body)
            n.value = base + LINKS * PAIRS

        def tensor_nodes(pe):
            def body(k, o, rows):
                q = k * 2 + o
                wait(pe, h_ready, q + 1)
                wait(pe, hT_ready, q - 1)
                for t in range(2):
                    for c in range(2):
                        last = nc.tensor.transpose(banks[o][:, (2 * t + c) * P:(2 * t + c + 1) * P],
                                                   nh[:, o, t, c * P:(c + 1) * P], ident[:, :])
                last.then_inc(hT_in_psum, 1)
                wait(pe, hT_ready, q + 1)
                wait(pe, lr_ready, (q - 1) * 4)
                for t in range(2):
                    bank = banks[2 + 2 * o + t]
                    for c in range(2):
                        nc.tensor.matmul(bank[:, :], nhT[:, o, t, c * P:(c + 1) * P], wlr_sb[:, c, :],
                                         start=(c == 0), stop=False)
                    nc.tensor.matmul(bank[:, :], ones[0:1, :], blr_sb[0:1, :],
                                     start=False, stop=True).then_inc(lr_in_psum, 1)
            pe.wait_ge(s_weights, WEIGHTS)
            run_pairs(pe, body)
            pe.wait_ge(hT_ready, PAIRS)
            pe.wait_ge(lr_ready, 4 * PAIRS)

        class Signals:
            def __init__(self, g):
                def s(name):
                    return sem(f"{name}_{g.name}")
                self.rec = [s(f"records_{o}") for o in range(UNROLL)]
                self.trow = [s(f"target_rows_{o}") for o in range(2)]
                self.tab = [s(f"gathered_{o}") for o in range(SLOTS)]
                self.onehot, self.ohT_psum, self.ohT = s("onehot"), s("onehotT_in_psum"), s("onehotT_ready")
                self.s_psum, self.relu, self.s_used = s("sum_in_psum"), s("relu_ready"), s("sum_used")
                self.split, self.m_psum, self.m_read = s("score_split"), s("masked_in_psum"), s("masked_read")
                self.new_max, self.me_psum, self.shifted = s("new_max"), s("edge_max_in_psum"), s("shifted")
                self.weight, self.rescale, self.pay = s("weight"), s("rescale"), s("weighted")
                self.agg_psum, self.agg_read = s("aggregate_in_psum"), s("aggregate_read")
                self.score = s("score_ready")

        sig = {}
        OHT, MISC = banks[0], banks[1]
        SUM, MASKED, AGG = banks[2:4], banks[4:6], banks[6:8]
        EDGE_MAX = MISC[:, 256:256 + GROUP * HEADS]

        def register_blocks(engine, g, first, count):
            _, regs = nc.values_load_multi_w_load_instructions(
                block_of[g][0:1, bass.ds(first, count)], engines=[engine], min_val=0,
                max_val=BLOCKS - 1, skip_runtime_bounds_check_because="block_of is at most BLOCKS - 1")
            return regs

        def sync_edges_loop(sp, g):
            s, (table, width) = sig[g], targets[g]

            def load(t):
                wait(sp, s.agg_psum, (t.g - (UNROLL - 1)) * GROUP)
                sp.dma_start(rec[:, t.rec, 0:GROUP * g.words],
                             records[g][:, bass.ds(t.g * (GROUP * g.words), GROUP * g.words)]
                             ).then_inc(s.rec[t.rec], 16)
                regs = register_blocks(mybir.EngineType.SP, g, t.g * GROUP, GROUP)
                wait(sp, s.s_psum, (t.g - 1) * 2)
                for j in range(GROUP):
                    sp.dma_start(trow[:, t.half, j * width:(j + 1) * width],
                                 table[bass.ds(regs[j] * P, P), :]).then_inc(s.trow[t.half], 16)
            run_all(sp, g.groups, load)

        def pool_edges_loop(pool, g):
            s = sig[g]

            def gather(t):
                o = t.slot
                pool.wait_ge(s.rec[t.rec], t.rec_uses * 16 + 16)
                wait(pool, s.agg_psum, (t.g - (SLOTS - 1)) * GROUP)
                settle(pool, s_settled)
                for j in range(GROUP):
                    nc.gpsimd.indirect_dma_start(
                        out=tab[:, o, j * g.width:(j + 1) * g.width], out_offset=None, in_=gathered[g],
                        in_offset=bass.IndirectOffsetOnAxis(ap=rec[:, t.rec, j * g.words:j * g.words + 1], axis=0)
                    ).then_inc(s.tab[o], 16)
            if g is G1:
                run_all(pool, g.groups, gather, lambda k, o: pool_scatter2(pool, k, o), SCATTER2_RUNS)
            else:
                run_all(pool, g.groups, gather)

        def tensor_edges_loop(pe, g):
            s = sig[g]
            is1 = g is G1
            width = targets[g][1]

            def transposes(t):
                o = t.slot
                wait(pe, s.onehot, t.g + 1)
                wait(pe, s.ohT, t.g * (3 if is1 else 2))
                wait(pe, s.shifted, t.g - 2)
                for j in range(GROUP):
                    last = nc.tensor.transpose(OHT[:, j * P:(j + 1) * P], oh[:, o, j, :], ident[:, :])
                if is1:
                    last = nc.tensor.transpose(MISC[0:GROUP * g.words, 0:P],
                                               rec[:, t.rec, 0:GROUP * g.words].bitcast(F32), ident[:, :])
                last.then_inc(s.ohT_psum, 1)

            def sums(t, half):
                o = t.slot
                wait(pe, s.s_used, t.g * 2 + (half - 1))
                if half == 0:
                    wait(pe, s.ohT, (t.g + 1) * (3 if is1 else 2))
                    wait(pe, s.trow[t.half], t.half_uses * 64 + 64)
                    if is1:
                        wait(pe, s.tab[o], t.uses * 64 + 64)
                for j in (2 * half, 2 * half + 1):
                    dst = SUM[half][:, (j % 2) * FEAT:(j % 2) * FEAT + width]
                    row = tab[:, o, j * g.width:(j + 1) * g.width]
                    last = nc.tensor.matmul(dst, ohT[:, o, j, :], trow[:, t.half, j * width:(j + 1) * width],
                                            start=True, stop=not is1)
                    if is1:
                        nc.tensor.matmul(dst, attrT[:, o, :], we_sb[:, j, :], start=False, stop=False)
                        row = row.rearrange("p (h d) -> p h d", h=HEADS)[:, :, 0:DIMS]
                        last = nc.tensor.matmul(dst, ident[:, :], row, start=False, stop=True)
                last.then_inc(s.s_psum, 1)

            def masked(t, tiles):
                o = t.slot
                wait(pe, s.split, t.g + 1)
                for j in tiles:
                    bank = MASKED[j % 2]
                    wait(pe, s.m_read, t.g * GROUP + (j - 1))
                    pj = pen[:, o, j * P:(j + 1) * P]
                    nc.tensor.matmul(bank[:, :].rearrange("p (h e) -> p h e", h=HEADS), ident_b[:, :],
                                     pj.unsqueeze(1).broadcast_to([P, HEADS, P]), start=True, stop=False)
                    for h in range(HEADS):
                        for half in (score_hi, score_lo):
                            c = j * HEADS + h
                            last = nc.tensor.matmul(bank[:, h * P:(h + 1) * P],
                                                    half[:, t.half, c:c + 1].broadcast_to([P, P]), ident_b[:, :],
                                                    start=False, stop=(h == HEADS - 1 and half is score_lo))
                    last.then_inc(s.m_psum, 1)

            def edge_max(t):
                o = t.slot
                wait(pe, s.new_max, t.g + 1)
                for j in range(GROUP):
                    c = slice(j * HEADS, (j + 1) * HEADS)
                    last = nc.tensor.matmul(EDGE_MAX[:, c], ohT[:, o, j, :], new_max[:, o, c], start=True, stop=True)
                last.then_inc(s.me_psum, 1)

            def aggregate(t, tiles):
                o = t.slot
                for j in tiles:
                    pe.wait_ge(s.pay, t.g * GROUP + (j + 1) if is1 else t.g + 1)
                    wait(pe, s.agg_read, t.g * GROUP + (j - 1))
                    last = nc.tensor.matmul(AGG[j % 2][:, 0:g.sums], oh[:, o, j, :],
                                            tab[:, o, j * g.width:j * g.width + g.sums], start=True, stop=True)
                    if is1:
                        e = rec[:, t.rec, j * g.words + 2:(j + 1) * g.words].bitcast(F32)
                        last = nc.tensor.matmul(AGG[j % 2][:, g.sums:g.acc], oh[:, o, j, :], e,
                                                start=True, stop=True, skip_group_check=True)
                    last.then_inc(s.agg_psum, 1)

            def body(t, left):
                start = isinstance(t.g, int) and t.g == 0
                masked(t, (0, 1))
                if is1:
                    if left >= 2:
                        transposes(t.near(2))
                    masked(t, (2, 3))
                else:
                    if not start:
                        edge_max(t.near(-1))
                    masked(t, (2, 3))
                    if left >= 2:
                        transposes(t.near(2))
                if not start:
                    aggregate(t.near(-1), (0, 1))
                if left >= 2:
                    sums(t.near(2), 0)
                if not start:
                    aggregate(t.near(-1), (2, 3))
                if left >= 2:
                    sums(t.near(2), 1)
                if is1:
                    edge_max(t)
            for g0 in (0, 1):
                transposes(step_of(g0))
                sums(step_of(g0), 0)
                sums(step_of(g0), 1)
            run_groups(pe, g.groups, body)
            if not is1:
                edge_max(step_of(g.groups - 1))
            aggregate(step_of(g.groups - 1), range(GROUP))

        def scalar_edges_loop(act, g):
            s = sig[g]
            is1 = g is G1

            def copies(t):
                o = t.slot
                wait(act, s.ohT_psum, t.g + 1)
                wait(act, s.me_psum, t.g - (SLOTS - 1))
                nc.scalar.copy(ohT[:, o, :, :].rearrange("p j e -> p (j e)"), OHT[:, :]).then_inc(s.ohT, 1)
                nc.scalar.activation(pen[:, o, :], OHT[:, :], ACT.Copy, bias=NEG, scale=-NEG).then_inc(s.ohT, 1)
                if is1:
                    nc.scalar.copy(attrT[:, o, :], MISC[0:GROUP * G1.words, 0:P]).then_inc(s.ohT, 1)

            def relus(t):
                wait(act, s.score, t.g)
                for q in range(2):
                    wait(act, s.s_psum, t.g * 2 + (q + 1))
                    nc.scalar.activation(relu[:, q * 512:(q + 1) * 512], SUM[q][:, :], ACT.Relu,
                                         scale=1.0 - SLOPE).then_inc(s.relu, 1)

            def weights(t, between):
                wait(act, s.shifted, t.g + 1)
                nc.scalar.activation(weight[:, :], shifted[:, :], ACT.Exp).then_inc(s.weight, 1)
                if is1:
                    wait(act, s.weight, t.g + 1)
                    for j in range(GROUP):
                        for h in range(HEADS):
                            c = j * g.width + h * (g.dims + 1)
                            row = tab[:, t.slot, c:c + g.dims + 1]
                            last = nc.scalar.activation(row, row, ACT.Copy,
                                                        scale=weight[:, j * HEADS + h:j * HEADS + h + 1])
                        last.then_inc(s.pay, 1)
                        if j == 1:
                            between()
                else:
                    between()

            def rescales(t):
                wait(act, s.new_max, t.g + 1)
                nc.scalar.activation(rescale[:, t.slot, :], fall[:, t.slot, :], ACT.Exp).then_inc(s.rescale, 1)

            def body(t, left):
                if left >= 1 and is1:
                    relus(t.near(1))
                if not (isinstance(t.g, int) and t.g == 0):
                    weights(t.near(-1), lambda: left >= 2 and copies(t.near(2)))
                elif left >= 2:
                    copies(t.near(2))
                rescales(t)
            copies(step_of(0))
            if is1:
                relus(step_of(0))
            copies(step_of(1))
            run_groups(act, g.groups, body)
            weights(step_of(g.groups - 1), lambda: None)

        def vector_edges_loop(v, g, n):
            s = sig[g]
            is1 = g is G1
            acc, mx = accs[g], maxs[g]
            base = n.value

            def onehots(t):
                o = t.slot
                v.wait_ge(s.rec[t.rec], t.rec_uses * 16 + 16)
                wait(v, s.agg_psum, (t.g - (SLOTS - 1)) * GROUP)
                w = rec[:, t.rec, 0:GROUP * g.words].bitcast(F32).rearrange("p (j w) -> p j w", w=g.words)[:, :, 1:2]
                nc.vector.tensor_tensor(oh[:, o, :, :], iota[:, :].unsqueeze(1).broadcast_to([P, GROUP, P]),
                                        w.broadcast_to([P, GROUP, P]), ALU.is_equal).then_inc(s.onehot, 1)

            def shift(t):
                wait(v, s.me_psum, t.g + 1)
                nc.vector.tensor_tensor(shifted[:, :], score[:, t.slot, :], EDGE_MAX, ALU.subtract).then_inc(s.shifted, 1)

            def lrelu(t, q):
                if is1:
                    wait(v, s.relu, t.g * 2 + (q + 1))
                    c = slice(q * 512, (q + 1) * 512)
                    last = nc.vector.scalar_tensor_tensor(relu[:, c], SUM[q][:, :], SLOPE, relu[:, c],
                                                          ALU.mult, ALU.add)
                else:
                    wait(v, s.s_psum, t.g * 2 + (q + 1))
                    if q == 0:
                        wait(v, s.tab[t.slot], t.uses * 64 + 64)
                    rows = tab[:, t.slot, 0:GROUP * g.width].rearrange("p (j w) -> p j w", w=g.width)
                    last = nc.vector.tensor_tensor(
                        score[:, t.slot, q * 8:(q + 1) * 8].rearrange("p (j h) -> p j h", h=HEADS),
                        SUM[q][:, :].rearrange("p (j f) -> p j f", f=FEAT)[:, :, 0:HEADS],
                        rows[:, 2 * q:2 * q + 2, g.sums:g.sums + HEADS], ALU.add)
                last.then_inc(s.s_used, 1)

            def weigh(t):
                wait(v, s.s_used, t.g * 2 + 2)
                if is1:
                    l4 = relu[:, :].rearrange("p (j f) -> p j f", f=FEAT)
                    n.add(nc.vector.tensor_tensor(l4, l4, att_sb[:, :].unsqueeze(1).broadcast_to([P, GROUP, FEAT]),
                                                  ALU.mult))
                else:
                    sc = score[:, t.slot, :]
                    n.add(nc.vector.scalar_tensor_tensor(sc, sc, SLOPE, sc, ALU.mult, ALU.max))

            def total(t):
                sc = score[:, t.slot, :]
                if is1:
                    n.link(nc.vector.tensor_reduce(sc, relu[:, :].rearrange("p (c d) -> p c d", d=DIMS), AX.X,
                                                   ALU.add))
                wait(v, s.m_psum, (t.g - 1) * GROUP)
                nc.vector.tensor_copy(score_hi[:, t.half, :], sc).then_inc(s.score, 1)

            def split(t):
                wait(v, s.score, t.g + 1)
                nc.vector.tensor_tensor(score_lo[:, t.half, :], score[:, t.slot, :], score_hi[:, t.half, :],
                                        ALU.subtract).then_inc(s.split, 1)

            def weighted(t):
                o = t.slot
                wait(v, s.weight, t.g + 1)
                rows = tab[:, o, 0:GROUP * g.width].rearrange("p (j w) -> p j w", w=g.width)[:, :, 0:g.sums]
                rows = rows.rearrange("p j (h d) -> p j h d", h=HEADS)
                wt = weight[:, :].rearrange("p (j h) -> p j h", h=HEADS).unsqueeze(3).broadcast_to(
                    [P, GROUP, HEADS, g.dims + 1])
                nc.vector.tensor_tensor(rows, rows, wt, ALU.mult).then_inc(s.pay, 1)

            def tile_max(t, tiles):
                for j in tiles:
                    wait(v, s.m_psum, t.g * GROUP + (j + 1))
                    nc.vector.tensor_reduce(tmax[:, j, :], MASKED[j % 2][:, :].rearrange("p (h e) -> p h e", h=HEADS),
                                            AX.X, ALU.max).then_inc(s.m_read, 1)

            def accumulate(t, regs, j):
                o = t.slot
                wait(v, s.rescale, t.g + 1)
                wait(v, s.agg_psum, t.g * GROUP + (j + 1))
                wait(v, s.agg_read, t.g * GROUP + j)
                a = acc[:, bass.ds(regs[j], 1), :].rearrange("p a n -> p (a n)")
                bank = AGG[j % 2]
                if is1:
                    w = g.dims + 1
                    for h in range(HEADS):
                        c = slice(h * w, (h + 1) * w)
                        r = rescale[:, o, j * HEADS + h:j * HEADS + h + 1]
                        nc.vector.scalar_tensor_tensor(a[:, c], a[:, c], r, bank[:, c], ALU.mult, ALU.add)
                    c = slice(g.sums, g.acc)
                    last = nc.vector.tensor_tensor(a[:, c], a[:, c], bank[:, c], ALU.add)
                else:
                    r = rescale[:, o, j * HEADS:(j + 1) * HEADS].unsqueeze(2).broadcast_to([P, HEADS, g.dims + 1])
                    a3 = a.rearrange("p (h d) -> p h d", h=HEADS)
                    n.link(nc.vector.tensor_tensor(a3, a3, r, ALU.mult))
                    last = nc.vector.tensor_tensor(a, a, bank[:, 0:g.sums], ALU.add)
                last.then_inc(s.agg_read, 1)

            def maximum(t, regs, j):
                wait(v, s.m_read, t.g * GROUP + (j + 1))
                m = mx[:, bass.ds(regs[j], 1), :].rearrange("p a n -> p (a n)")
                nc.vector.tensor_scalar(old_max[:, j, :], m, 1.0, None, ALU.mult)
                nc.vector.tensor_tensor(new_max[:, t.slot, j * HEADS:(j + 1) * HEADS], m, tmax[:, j, :], ALU.max)
                n.add(nc.vector.tensor_tensor(m, m, tmax[:, j, :], ALU.max))

            def falls(t):
                nc.vector.tensor_tensor(fall[:, t.slot, :], old_max[:, :, :].rearrange("p j h -> p (j h)"),
                                        new_max[:, t.slot, :], ALU.subtract).then_inc(s.new_max, 1)

            def maxima_and_scores(t, regs, before_regs, more):
                wait(v, s.me_psum, t.g - (SLOTS - 1))
                wait(v, s.rescale, t.g - (SLOTS - 1))
                u = t.near(1)

                def add(j):
                    if before_regs:
                        accumulate(t.near(-1), before_regs, j)
                maximum(t, regs, 0)
                if more and is1:
                    lrelu(u, 1)
                n.wait()
                maximum(t, regs, 1)
                add(0)
                n.wait()
                maximum(t, regs, 2)
                add(1)
                n.wait()
                maximum(t, regs, 3)
                if more and is1:
                    weigh(u)
                add(2)
                n.wait()
                falls(t)
                if more and is1:
                    total(u)
                    split(u)
                add(3)

            ACC_LINKS = 0 if is1 else GROUP
            SCORE_LINKS = 2 if is1 else 1
            PER = SCORE_LINKS + ACC_LINKS + GROUP

            def body(t, left):
                start = isinstance(t.g, int) and t.g == 0
                n.value = base + SCORE_LINKS if start else base + SCORE_LINKS - ACC_LINKS + t.g * PER
                if start:
                    regs, before_regs = list(register_blocks(mybir.EngineType.DVE, g, 0, GROUP)), None
                else:
                    r8 = register_blocks(mybir.EngineType.DVE, g, (t.g - 1) * GROUP, 2 * GROUP)
                    before_regs, regs = list(r8)[:GROUP], list(r8)[GROUP:]
                if is1 and not start:
                    shift(t.near(-1))
                tile_max(t, (0, 1))
                if not is1 and not start:
                    shift(t.near(-1))
                if left >= 1:
                    lrelu(t.near(1), 0)
                if is1:
                    tile_max(t, (2, 3))
                else:
                    if left >= 1:
                        lrelu(t.near(1), 1)
                    tile_max(t, (2,))
                    if left >= 1:
                        weigh(t.near(1))
                    tile_max(t, (3,))
                    if left >= 1:
                        n.wait()
                        total(t.near(1))
                    if not start:
                        weighted(t.near(-1))
                    if left >= 1:
                        split(t.near(1))
                maxima_and_scores(t, regs, before_regs, left >= 1)
                if left >= 3:
                    onehots(t.near(3))
            for g0 in range(3):
                onehots(step_of(g0))
            first = step_of(0)
            lrelu(first, 0)
            lrelu(first, 1)
            weigh(first)
            n.wait()
            total(first)
            split(first)
            run_groups(v, g.groups, body)
            n.value = base - ACC_LINKS + g.groups * PER
            t = step_of(g.groups - 1)
            shift(t)
            if not is1:
                weighted(t)
            regs = list(register_blocks(mybir.EngineType.DVE, g, (g.groups - 1) * GROUP, GROUP))
            for j in range(GROUP):
                accumulate(t, regs, j)
            v.wait_ge(s.agg_read, g.groups * GROUP)

        fin_loaded = [sem("node_rows_loaded_a"), sem("node_rows_loaded_b")]
        mean_attr, mean_attr_psum, mean_attr_T = sem("mean_attr"), sem("mean_attr_in_psum"), sem("mean_attr_T")
        self_sum = sem("self_attr_in_psum")
        self_fall, self_exp = sem("self_fall"), sem("self_exp")
        layer_out, tanh_out = sem("layer_output"), sem("tanh_of_output")
        x1_ready, x1_stored = sem("x1_ready"), [sem("x1_stored_a"), sem("x1_stored_b")]
        z_ready, z_psum, z_copied = sem("z_ready"), sem("z_in_psum"), sem("z_copied")
        zg_psum, zg_copied = sem("zg_in_psum"), sem("zg_copied")
        gate_rows_ready, gate_rows_stored = sem("gate_rows_ready"), sem("gate_rows_stored")
        GATE_STORES = 32

        def sync_finish(sp):
            def body(k, o, rows):
                q = k * 2 + o
                wait(sp, x1_ready, q - 1)
                sp.dma_start(nxl[:, o, :, :], pair_rows(xl_table, q)).then_inc(fin_loaded[o], 16)
                sp.dma_start(nxr[:, o, :, :], pair_rows(xr_table, q)).then_inc(fin_loaded[o], 16)
                sp.dma_start(nxh[:, o, :, :], pair_rows(xh_table, q)).then_inc(fin_loaded[o], 16)
            sp.wait_ge(summed1, 1)
            run_pairs(sp, body)
            sp.wait_ge(gate_rows_ready, 1)
            sp.dma_start(gate_table[0:NODES_PAD, :].rearrange("(b p) w -> p b w", p=P),
                         gate_rows[:, :, :]).then_inc(gate_rows_stored, 16)
            sp.dma_start(adst_table[:, :].rearrange("(b p) w -> p b w", p=P), adst).then_inc(gate_rows_stored, 16)

        def scalar_finish(act):
            def mean(q, o):
                wait(act, mean_attr_psum, q + 1)
                nc.scalar.copy(laT, banks[o][0:2 + EDGE_DIM, 0:2 * P]).then_inc(mean_attr_T, 1)

            def body(k, o, rows):
                q = k * 2 + o
                wait(act, self_fall, q + 1)
                nc.scalar.activation(small[:, :, 40:48], small[:, :, 32:40], ACT.Exp).then_inc(self_exp, 1)
                if rows == P:
                    mean(q + 1, 1 - o)
                wait(act, layer_out, q + 1)
                nc.scalar.activation(flat(nx[:, o, :, :]), flat(nh[:, o, :, :]), ACT.Tanh,
                                     scale=0.5).then_inc(tanh_out, 1)
                wait(act, x1_ready, q + 1)
                act.dma_start(pair_rows(x1_table, q), nh[:, o, :, :]).then_inc(x1_stored[o], 16)
                wait(act, z_psum, q + 1)
                nc.scalar.copy(flat(nhT[:, o, :, :]), banks[o][:, :]).then_inc(z_copied, 1)
                nc.scalar.copy(zT[:, bass.ds(q * 2, 2), :],
                               banks[o][:, :].rearrange("p (t f) -> p t f", t=2)).then_inc(z_copied, 1)
                wait(act, zg_psum, q + 1)
                nc.scalar.copy(zg[:, bass.ds(q * 2, 2), :],
                               banks[4 + o][:, 0:2 * GAT].rearrange("p (t f) -> p t f", t=2)).then_inc(zg_copied, 1)
            mean(0, 0)
            run_pairs(act, body)

        def tensor_finish(pe):
            def mean(q, o):
                wait(pe, mean_attr, q + 1)
                wait(pe, z_copied, (q - 1) * 2)
                for t in range(2):
                    last = nc.tensor.transpose(banks[o][0:2 + EDGE_DIM, t * P:(t + 1) * P],
                                               small[:, t, 0:2 + EDGE_DIM], ident[:, :])
                last.then_inc(mean_attr_psum, 1)
                wait(pe, mean_attr_T, q + 1)
                for t in range(2):
                    last = nc.tensor.matmul(banks[2 + o][:, t * FEAT:(t + 1) * FEAT], laT[:, t * P:(t + 1) * P],
                                            we_sb[0:2 + EDGE_DIM, 0, :], start=True, stop=True)
                last.then_inc(self_sum, 1)

            def body(k, o, rows):
                q = k * 2 + o
                if rows == P:
                    mean(q + 1, 1 - o)
                wait(pe, z_ready, q + 1)
                for t in range(2):
                    for c in range(2):
                        last = nc.tensor.transpose(banks[o][:, (2 * t + c) * P:(2 * t + c + 1) * P],
                                                   nx[:, o, t, c * P:(c + 1) * P], ident[:, :])
                last.then_inc(z_psum, 1)
                wait(pe, z_copied, q * 2 + 2)
                for t in range(2):
                    for c in range(2):
                        last = nc.tensor.matmul(banks[4 + o][:, t * GAT:(t + 1) * GAT],
                                                nhT[:, o, t, c * P:(c + 1) * P], wgat_sb[:, c, :],
                                                start=(c == 0), stop=(c == 1))
                last.then_inc(zg_psum, 1)
            mean(0, 0)
            run_pairs(pe, body)

        def pool_rstd(pool):
            with pool.Fori(0, PAIRS) as q:
                pool.wait_ge(rstd_in, q + 1)
                nc.gpsimd.tensor_tensor(rstd[:, 0, :], variance[:, 0, :], neg_half[:, 0:2],
                                        ALU.pow).then_inc(rstd_out, 1)

        def vector_finish(v, n):
            n.link(nc.vector.memset(small[:, :, :], 0.0))
            v.sem_inc(summed1, 1)
            base = n.value
            LINKS = 21

            def heads(a):
                return a.rearrange("p t (h d) -> p t h d", h=HEADS)

            def mean(q):
                a = acc1[:, bass.ds(q * 2, 2), :]

                def col(c, width):
                    return small[:, :, c:c + width]
                n.link(nc.vector.tensor_scalar(col(20, 1), a[:, :, G1.acc - 1:G1.acc], 1.0, None, ALU.max))
                n.link(nc.vector.reciprocal(col(21, 1), col(20, 1)))
                nc.vector.tensor_tensor(col(2, EDGE_DIM), a[:, :, G1.sums:G1.sums + EDGE_DIM],
                                        col(21, 1).broadcast_to([P, 2, EDGE_DIM]), ALU.mult).then_inc(mean_attr, 1)

            def body(k, o, rows):
                q = k * 2 + o
                n.value = base + 2 + q * LINKS
                a = acc1[:, bass.ds(q * 2, 2), :]
                m = max1[:, bass.ds(q * 2, 2), :]
                xl, xr, xh, s = nxl[:, o, :, :], nxr[:, o, :, :], nxh[:, o, :, :], nh[:, o, :, :]

                def col(c, width=HEADS):
                    return small[:, :, c:c + width]
                v.wait_ge(fin_loaded[o], k * 48 + 48)
                wait(v, x1_stored[o], k * 16)
                wait(v, self_sum, q + 1)
                n.link(nc.vector.tensor_tensor(s, banks[2 + o][:, :].rearrange("p (t f) -> p t f", t=2), xr, ALU.add))
                n.link(nc.vector.tensor_tensor(heads(s), heads(s), heads(xl)[:, :, :, 0:DIMS], ALU.add))
                n.link(nc.vector.scalar_tensor_tensor(s, s, SLOPE, s, ALU.mult, ALU.max))
                n.link(nc.vector.tensor_tensor(s, s, att_sb[:, :].unsqueeze(1).broadcast_to([P, 2, FEAT]), ALU.mult))
                n.link(nc.vector.tensor_reduce(col(24), heads(s), AX.X, ALU.add))
                n.link(nc.vector.tensor_tensor(col(28), m, col(24), ALU.max))
                n.add(nc.vector.tensor_tensor(col(32), m, col(28), ALU.subtract))
                nc.vector.tensor_tensor(col(36), col(24), col(28), ALU.subtract).then_inc(self_fall, 1)
                if rows == P:
                    mean(q + 1)
                wait(v, self_exp, q + 1)

                def per_head(c, width):
                    return col(c).unsqueeze(3).broadcast_to([P, 2, HEADS, width])
                a4 = heads(a[:, :, 0:G1.sums])
                n.add(nc.vector.tensor_tensor(a4, a4, per_head(40, DIMS + 1), ALU.mult))
                n.link(nc.vector.tensor_tensor(heads(xl), heads(xl), per_head(44, DIMS + 1), ALU.mult))
                n.link(nc.vector.tensor_tensor(a4, a4, heads(xl), ALU.add))
                n.link(nc.vector.tensor_scalar(col(48), a4[:, :, :, DIMS], 1.0e-16, None, ALU.add))
                n.link(nc.vector.reciprocal(col(52), col(48)))
                n.link(nc.vector.tensor_tensor(heads(s), a4[:, :, :, 0:DIMS], per_head(52, DIMS), ALU.mult))
                nc.vector.tensor_tensor(s, s, bias_sb[:, :].unsqueeze(1).broadcast_to([P, 2, FEAT]),
                                        ALU.add).then_inc(layer_out, 1)
                e = nx[:, o, :, :]
                wait(v, tanh_out, q + 1)
                n.link(nc.vector.tensor_scalar(e, e, 0.5, 0.5, ALU.mult, ALU.add))
                n.link(nc.vector.tensor_tensor(s, s, e, ALU.mult))
                nc.vector.tensor_tensor(s, s, xh, ALU.add).then_inc(x1_ready, 1)
                wait(v, x1_ready, q + 1)
                n.add(nc.vector.bn_stats(stats[:, 0, :], nh[:, o, 0, :]))
                n.link(nc.vector.bn_stats(stats[:, 1, :], nh[:, o, 1, :]))
                settle(v, s_settled)
                n.add(nc.vector.bn_aggr(mv[:, o, 0, :], stats[:, 0, :]))
                n.link(nc.vector.bn_aggr(mv[:, o, 1, :], stats[:, 1, :]))
                nc.vector.tensor_scalar(variance[:, 0, :], mv[:, o, :, 1], EPS, None, ALU.add).then_inc(rstd_in, 1)
                wait(v, rstd_out, q + 1)
                for t in range(2):
                    last = nc.vector.tensor_scalar(nx[:, o, t, :], nh[:, o, t, :], mv[:, o, t, 0:1],
                                                   rstd[:, 0, t:t + 1], ALU.subtract, ALU.mult)
                last.then_inc(z_ready, 1)
                assert not isinstance(k, int) or rows != P or n.value == base + 2 + (q + 1) * LINKS, n.value - base
            mean(0)
            run_pairs(v, body)
            n.value = base + PAIRS * LINKS
            v.wait_ge(zg_copied, PAIRS)
            v.wait_ge(z_copied, 2 * PAIRS)
            v.wait_ge(x1_stored[0], 16 * (PAIRS // 2 + 1))
            v.wait_ge(x1_stored[1], 16 * (PAIRS // 2))
            v.wait_ge(scattered2, 16 * G2.cols)
            used[0] = 0
            t = wide_part(BLOCKS, GAT)
            z4 = zg.rearrange("p b (h e) -> p b h e", h=HEADS)
            g4 = gate_rows[:, :, 0:G2.sums].rearrange("p b (h d) -> p b h d", h=HEADS)
            n.link(nc.vector.memset(gate_rows[:, :, :], 1.0))
            for h in range(HEADS):
                n.add(nc.vector.tensor_copy(g4[:, :, h, 0:EXPERTS], z4[:, :, h, :]))
            for c, to in ((0, gate_rows[:, :, G2.sums:G2.width]), (1, adst)):
                n.link(nc.vector.tensor_tensor(t, zg, gat_consts[:, c, :].unsqueeze(1).broadcast_to([P, BLOCKS, GAT]),
                                               ALU.mult))
                n.link(nc.vector.tensor_reduce(to, t.rearrange("p b (h e) -> p b h e", h=HEADS), AX.X, ALU.add))
            n.link(nc.vector.memset(acc2[:, :, :], 0.0))
            nc.vector.memset(max2[:, :, :], NEG).then_inc(gate_rows_ready, 1)
            v.wait_ge(gate_rows_ready, 1)
            v.wait_ge(gate_rows_stored, GATE_STORES)

        gate_exp_in, gate_exp_out = sem("gate_exp_in"), sem("gate_exp_out")
        gates_ready = sem("gates_ready")
        gates = sb("gates", [P, BLOCKS, EXPERTS])
        used[0] = 0
        q_score = wide_part(BLOCKS, HEADS)
        q_max = wide_part(BLOCKS, HEADS)
        q_fall = wide_part(2, BLOCKS, HEADS)
        q_rows = wide_part(BLOCKS, G2.sums)
        q_agg = wide_part(BLOCKS, GAT)
        q_sq = wide_part(BLOCKS, GAT)
        q_mean = wide_part(BLOCKS)
        q_var = wide_part(BLOCKS)
        q_rank = wide_part(BLOCKS, EXPERTS)
        q_cmp = wide_part(BLOCKS)

        def vector_gates(v, n):
            def b3(a, w):
                return a.unsqueeze(2).broadcast_to([P, BLOCKS, w])
            link = n.link
            link(nc.vector.tensor_tensor(q_score, gate_rows[:, :, G2.sums:G2.width], adst, ALU.add))
            link(nc.vector.scalar_tensor_tensor(q_score, q_score, SLOPE, q_score, ALU.mult, ALU.max))
            link(nc.vector.tensor_tensor(q_max, max2[:, :, :], q_score, ALU.max))
            n.add(nc.vector.tensor_tensor(q_fall[:, 0], max2[:, :, :], q_max, ALU.subtract))
            nc.vector.tensor_tensor(q_fall[:, 1], q_score, q_max, ALU.subtract).then_inc(gate_exp_in, 1)
            v.wait_ge(gate_exp_out, 1)
            acc = acc2[:, :, :].rearrange("p b (h d) -> p b h d", h=HEADS)
            rows = gate_rows[:, :, 0:G2.sums].rearrange("p b (h d) -> p b h d", h=HEADS)
            qr = q_rows.rearrange("p b (h d) -> p b h d", h=HEADS)
            wide5 = [P, BLOCKS, HEADS, EXPERTS + 1]
            n.add(nc.vector.tensor_tensor(acc, acc, q_fall[:, 0].unsqueeze(3).broadcast_to(wide5), ALU.mult))
            link(nc.vector.tensor_tensor(qr, rows, q_fall[:, 1].unsqueeze(3).broadcast_to(wide5), ALU.mult))
            link(nc.vector.tensor_tensor(acc2[:, :, :], acc2[:, :, :], q_rows, ALU.add))
            link(nc.vector.tensor_scalar(q_score, acc[:, :, :, EXPERTS], 1.0e-16, None, ALU.add))
            link(nc.vector.reciprocal(q_max, q_score))
            agg = q_agg.rearrange("p b (h d) -> p b h d", h=HEADS)
            link(nc.vector.tensor_tensor(agg, acc[:, :, :, 0:EXPERTS],
                                         q_max.unsqueeze(3).broadcast_to([P, BLOCKS, HEADS, EXPERTS]), ALU.mult))

            def const(c):
                return gat_consts[:, c, :].unsqueeze(1).broadcast_to([P, BLOCKS, GAT])
            link(nc.vector.tensor_tensor(q_agg, q_agg, const(2), ALU.add))
            link(nc.vector.tensor_reduce(q_mean, q_agg, AX.X, ALU.add))
            link(nc.vector.tensor_scalar(q_mean, q_mean, 1.0 / GAT, None, ALU.mult))
            link(nc.vector.tensor_tensor(q_agg, q_agg, b3(q_mean, GAT), ALU.subtract))
            link(nc.vector.tensor_tensor(q_sq, q_agg, q_agg, ALU.mult))
            link(nc.vector.tensor_reduce(q_var, q_sq, AX.X, ALU.add))
            nc.vector.tensor_scalar(q_mean, q_var, 1.0 / GAT, EPS, ALU.mult, ALU.add).then_inc(rstd_in, 1)
            v.wait_ge(rstd_out, PAIRS + 1)
            link(nc.vector.tensor_tensor(q_agg, q_agg, b3(q_var, GAT), ALU.mult))
            link(nc.vector.tensor_tensor(q_agg, q_agg, const(3), ALU.mult))
            link(nc.vector.tensor_tensor(q_agg, q_agg, const(4), ALU.add))
            link(nc.vector.tensor_reduce(q_score, q_agg.rearrange("p b (h e) -> p b e h", h=HEADS), AX.X, ALU.add))
            link(nc.vector.tensor_scalar(q_score, q_score, 1.0 / HEADS, None, ALU.mult))
            link(nc.vector.memset(q_rank, 0.0))
            for i in range(EXPERTS):
                for j in range(i + 1, EXPERTS):
                    link(nc.vector.tensor_tensor(q_cmp, q_score[:, :, j], q_score[:, :, i], ALU.is_gt))
                    link(nc.vector.tensor_tensor(q_rank[:, :, i], q_rank[:, :, i], q_cmp, ALU.add))
                    link(nc.vector.tensor_tensor(q_cmp, q_score[:, :, i], q_score[:, :, j], ALU.is_ge))
                    link(nc.vector.tensor_tensor(q_rank[:, :, j], q_rank[:, :, j], q_cmp, ALU.add))
            link(nc.vector.tensor_reduce(q_mean, q_score, AX.X, ALU.max))
            nc.vector.tensor_tensor(q_score, q_score, b3(q_mean, EXPERTS), ALU.subtract).then_inc(gate_exp_in, 1)
            v.wait_ge(gate_exp_out, 2)
            link(nc.vector.scalar_tensor_tensor(q_score, q_rank, 2.0, q_max, ALU.is_lt, ALU.mult))
            link(nc.vector.tensor_reduce(q_mean, q_score, AX.X, ALU.add))
            link(nc.vector.reciprocal(q_var, q_mean))
            nc.vector.tensor_tensor(gates[:, :, :], q_score, b3(q_var, EXPERTS), ALU.mult).then_inc(gates_ready, 1)
            v.wait_ge(gates_ready, 1)

        def scalar_gates(act):
            act.wait_ge(gate_exp_in, 1)
            nc.scalar.activation(q_fall, q_fall, ACT.Exp).then_inc(gate_exp_out, 1)
            act.wait_ge(gate_exp_in, 2)
            nc.scalar.activation(q_max, q_score, ACT.Exp).then_inc(gate_exp_out, 1)

        used[0] = 0
        w1_sb = wide_part(EXPERTS, 2, HIDDEN)
        w2_sb = wide_part(EXPERTS, 4, FEAT)
        hid = wide_part(2, 4, 2 * P)
        b1_sb = sb("b1_sb", [P, EXPERTS, 4])
        b2_sb = sb("b2_sb", [EXPERTS, FEAT])
        x1_t = staged_attr[:, :, :].rearrange("p o n -> p (o n)")[:, 0:4 * FEAT].rearrange(
            "p (o t f) -> p o t f", o=2, t=2)
        out_t = staged_rec[:, :, :].rearrange("p o n -> p (o n)")[:, 0:4 * FEAT].bitcast(F32).rearrange(
            "p (o t f) -> p o t f", o=2, t=2)
        gate_t = sb("gate_t", [P, 2, 2, EXPERTS])
        gateT = attrT[:, :, :].rearrange("p o n -> p (o n)")[0:EXPERTS, 0:2 * P]
        w_loaded = sem("expert_weights_loaded")
        EXPERT_WEIGHTS = 64
        x1_loaded = [sem("x1_loaded_a"), sem("x1_loaded_b")]
        gate_copied, gateT_psum, gateT_ready = sem("gate_copied"), sem("gateT_in_psum"), sem("gateT_ready")
        b2_psum, started = sem("b2_in_psum"), sem("output_started")
        hid_psum, hid_ready = sem("hidden_in_psum"), sem("hidden_ready")
        y_psum, y_added = sem("expert_in_psum"), sem("expert_added")
        stored = [sem("stored_a"), sem("stored_b")]

        def sync_experts(sp):
            sp.wait_ge(gates_ready, 1)
            sp.dma_start(w1_sb, w1.rearrange("e (k p) n -> p e k n", p=P)).then_inc(w_loaded, 16)
            sp.dma_start(w2_sb, w2.rearrange("e (c p) n -> p e c n", p=P)).then_inc(w_loaded, 16)
            sp.dma_start(b1_sb[:, :, :], b1.rearrange("p (e c) -> p e c", e=EXPERTS)).then_inc(w_loaded, 16)
            sp.dma_start(b2_sb[:, :], b2).then_inc(w_loaded, 16)

            def body(k, o, rows):
                q = k * 2 + o
                sp.wait_ge(started, q + 1)
                sp.dma_start(x1_t[:, o, :, :], x1_table[bass.ds(q * (2 * P), 2 * P), :].rearrange(
                    "(t p) f -> p t f", p=P)).then_inc(x1_loaded[o], 16)
            run_pairs(sp, body)

        def scalar_experts(act):
            act.wait_ge(w_loaded, EXPERT_WEIGHTS)

            def body(k, o, rows):
                q = k * 2 + o
                act.wait_ge(gateT_psum, q + 1)
                nc.scalar.copy(gateT, banks[7][0:EXPERTS, 0:2 * P]).then_inc(gateT_ready, 1)
                for e in range(EXPERTS):
                    act.wait_ge(y_psum, q * EXPERTS + (e + 1))
                    for c in range(4):
                        act.wait_ge(hid_psum, q * 16 + (e * 4 + c + 1))
                        nc.scalar.activation(hid[:, e % 2, c, :], banks[c][:, 0:2 * P], ACT.Gelu,
                                             bias=b1_sb[:, e, c:c + 1]).then_inc(hid_ready, 1)
            run_pairs(act, body)

        def tensor_experts(pe):
            pe.wait_ge(w_loaded, EXPERT_WEIGHTS)
            pe.sem_inc(y_psum, 2)

            def body(k, o, rows):
                q = k * 2 + o
                pe.wait_ge(gate_copied, q + 1)
                for t in range(2):
                    last = nc.tensor.transpose(banks[7][0:EXPERTS, t * P:(t + 1) * P], gate_t[:, o, t, :], ident[:, :])
                last.then_inc(gateT_psum, 1)
                z = zT[:, bass.ds(q * 2, 2), :]

                def hidden(e):
                    for c in range(4):
                        i = e * 4 + c
                        pe.wait_ge(hid_ready, q * 16 + (i + 1))
                        for r in range(2):
                            last = nc.tensor.matmul(banks[c][:, 0:2 * P].rearrange("p (t n) -> p t n", t=2),
                                                    w1_sb[:, e, r, c * P:(c + 1) * P], z[:, :, r * P:(r + 1) * P],
                                                    start=(r == 0), stop=(r == 1))
                        last.then_inc(hid_psum, 1)

                def output(e):
                    pe.wait_ge(hid_ready, q * 16 + (e * 4 + 4 + 4))
                    pe.wait_ge(y_added, q * EXPERTS + (e + 1))
                    for t in range(2):
                        for c in range(4):
                            last = nc.tensor.matmul(banks[4 + e % 2][:, t * FEAT:(t + 1) * FEAT],
                                                    hid[:, e % 2, c, t * P:(t + 1) * P], w2_sb[:, e, c, :],
                                                    start=(c == 0), stop=(c == 3))
                    last.then_inc(y_psum, 1)
                hidden(0)
                pe.wait_ge(gateT_ready, q + 1)
                pe.wait_ge(started, q + 2)
                for t in range(2):
                    last = nc.tensor.matmul(banks[6][:, t * FEAT:(t + 1) * FEAT], gateT[:, t * P:(t + 1) * P],
                                            b2_sb[:, :], start=True, stop=True)
                last.then_inc(b2_psum, 1)
                hidden(1)
                output(0)
                hidden(2)
                output(1)
                hidden(3)
                output(2)
                output(3)
            run_pairs(pe, body)

        def vector_experts(v, n):
            v.sem_inc(started, 2)
            v.sem_inc(y_added, 2)
            v.sem_inc(hid_ready, 4)

            def body(k, o, rows):
                q = k * 2 + o
                g2 = gates[:, bass.ds(q * 2, 2), :]
                wait(v, stored[o], k * 32)
                settle(v, s_settled)
                nc.vector.tensor_copy(gate_t[:, o, :, :], g2).then_inc(gate_copied, 1)
                v.wait_ge(x1_loaded[o], k * 16 + 16)
                v.wait_ge(b2_psum, q + 1)
                nc.vector.tensor_tensor(out_t[:, o, :, :], banks[6][:, :].rearrange("p (t f) -> p t f", t=2),
                                        x1_t[:, o, :, :], ALU.add).then_inc(started, 1)
                v.wait_ge(started, q + 3)
                for e in range(EXPERTS):
                    v.wait_ge(y_psum, q * EXPERTS + (e + 3))
                    for t in range(2):
                        last = nc.vector.scalar_tensor_tensor(
                            out_t[:, o, t, :], banks[4 + e % 2][:, t * FEAT:(t + 1) * FEAT],
                            gate_t[:, o, t, e:e + 1], out_t[:, o, t, :], ALU.mult, ALU.add)
                    last.then_inc(y_added, 1)
                    v.wait_ge(y_added, q * EXPERTS + (e + 3))
            run_pairs(v, body)

        def pool_store(pool):
            def body(k, o, rows):
                q = k * 2 + o
                pool.wait_ge(y_added, q * EXPERTS + (EXPERTS + 2))
                for t in range(2):
                    r = rows if t else P
                    pool.dma_start(out[bass.ds(q * (2 * P) + t * P, r), :], out_t[0:r, o, t, :]).then_inc(stored[o], 16)
            run_pairs(pool, body)
            pool.wait_ge(stored[0], 32 * (PAIRS // 2 + 1))
            pool.wait_ge(stored[1], 32 * (PAIRS // 2))

        sig[G1] = Signals(G1)
        sig[G2] = Signals(G2)
        cleared = sem("sums_cleared")
        summed1 = sem("first_graph_summed")
        zero_rows_stored = sem("zero_rows_stored")

        @block.gpsimd
        def _(pool):
            n = pool_constants(pool)
            pool_fill(pool, n)
            pool_scatter1(pool, n)
            wait_nodes_stored(pool)
            pool.wait_ge(zero_rows_stored, 32)
            pool.wait_ge(held, 1)
            pool_edges_loop(pool, G1)
            pool_rstd(pool)
            pool.wait_ge(gate_rows_stored, GATE_STORES)
            pool_edges_loop(pool, G2)
            pool.wait_ge(rstd_in, PAIRS + 1)
            nc.gpsimd.tensor_tensor(q_var, q_mean, neg_half[:, :], ALU.pow).then_inc(rstd_out, 1)
            pool_store(pool)

        @block.sync
        def _(sp):
            sync_edges(sp, G1, src1, dst1)
            sync_edges(sp, G2, src2, dst2)
            sync_weights(sp)
            sync_fill(sp)
            sp.wait_ge(s_const, CONSTS)
            sp.dma_start(xl_table[ZERO_ROW:ZERO_ROW + 1, :], zero_row).then_inc(zero_rows_stored, 16)
            sp.dma_start(gate_table[ZERO_ROW:ZERO_ROW + 1, :], zero_row[:, 0:G2.width]).then_inc(zero_rows_stored, 16)
            sync_nodes(sp)
            sp.wait_ge(all_scattered[G1], 1)
            sp.wait_ge(blocks_ready[G1], 4)
            wait_nodes_stored(sp)
            sync_edges_loop(sp, G1)
            sync_finish(sp)
            sp.wait_ge(scattered2, 16 * G2.cols)
            sp.wait_ge(blocks_ready[G2], 3)
            sp.wait_ge(gate_rows_stored, GATE_STORES)
            sync_edges_loop(sp, G2)
            sync_experts(sp)

        @block.scalar
        def _(act):
            scalar_nodes(act)
            wait_nodes_stored(act)
            scalar_edges_loop(act, G1)
            scalar_finish(act)
            scalar_edges_loop(act, G2)
            scalar_gates(act)
            scalar_experts(act)

        @block.vector
        def _(v):
            n = Count(v, s_dve)
            nc.vector.memset(ones[:, :], 1.0).then_inc(s_const, 1)
            nc.vector.memset(we_sb[:, :, :], 0.0).then_inc(s_const, 1)
            v.wait_ge(s_const, 6)
            nc.vector.tensor_copy(ident_b[:, :], ident[:, :]).then_inc(s_const, 1)
            nc.vector.memset(zero_row, 0.0).then_inc(s_const, 1)
            vector_buckets(v, G1, n, True)
            vector_nodes(v, n)
            vector_buckets(v, G2, n, False)
            v.wait_ge(all_scattered[G1], 1)
            v.wait_ge(zero_rows_stored, 32)
            b = bucket[G2]
            n.add(nc.vector.tensor_copy(held_within, b["within"]))
            n.add(nc.vector.tensor_copy(held_slot, b["slot"]))
            n.link(nc.vector.tensor_copy(held_src, b["src"]))
            v.sem_inc(held, 1)
            nc.vector.memset(arena[:, :], 0.0).then_inc(cleared, 1)
            nc.vector.memset(max1[:, :, :], NEG).then_inc(cleared, 1)
            v.wait_ge(cleared, 2)
            wait_nodes_stored(v)
            vector_edges_loop(v, G1, n)
            vector_finish(v, n)
            vector_edges_loop(v, G2, n)
            vector_gates(v, n)
            vector_experts(v, n)

        @block.tensor
        def _(pe):
            pe.wait_ge(s_const, CONSTS)
            tensor_buckets(pe, G1, 0)
            tensor_nodes(pe)
            tensor_buckets(pe, G2, 1)
            tensor_edges_loop(pe, G1)
            tensor_finish(pe)
            tensor_edges_loop(pe, G2)
            tensor_experts(pe)


def kernel(x, src, dst, edge_attr_16, L0_gnn_W_l, L0_gnn_b_l, L0_gnn_W_r, L0_gnn_b_r, L0_gnn_W_e,
           L0_gnn_att, L0_gnn_bias, L0_ffn_W_gat, L0_ffn_att_src, L0_ffn_att_dst, L0_ffn_b_gat,
           L0_ffn_ln_gamma, L0_ffn_ln_beta, L0_ffn_W1, L0_ffn_b1, L0_ffn_W2, L0_ffn_b2,
           L0_ffn_edge_index):
    import numpy as np
    import concourse.bacc as bacc
    from concourse.bass_utils import run_bass_kernel_spmd

    def lay(a):
        return np.ascontiguousarray(np.asarray(a))

    arrays = {
        "x": lay(x), "src1": lay(src), "dst1": lay(dst), "attr": lay(edge_attr_16),
        "w_lr": lay(np.concatenate([np.asarray(L0_gnn_W_l).T, np.asarray(L0_gnn_W_r).T], axis=1)),
        "b_lr": lay(np.concatenate([np.asarray(L0_gnn_b_l), np.asarray(L0_gnn_b_r)])[None, :]),
        "w_e": lay(np.asarray(L0_gnn_W_e).T), "att": lay(np.asarray(L0_gnn_att).reshape(-1)),
        "bias": lay(L0_gnn_bias), "w_gat": lay(L0_ffn_W_gat),
        "att_src": lay(np.asarray(L0_ffn_att_src).reshape(-1)),
        "att_dst": lay(np.asarray(L0_ffn_att_dst).reshape(-1)), "b_gat": lay(L0_ffn_b_gat),
        "ln_gamma": lay(L0_ffn_ln_gamma), "ln_beta": lay(L0_ffn_ln_beta),
        "w1": lay(L0_ffn_W1), "b1": lay(np.asarray(L0_ffn_b1).reshape(EXPERTS * 4, P).T), "w2": lay(L0_ffn_W2), "b2": lay(L0_ffn_b2),
        "src2": lay(np.asarray(L0_ffn_edge_index)[0]), "dst2": lay(np.asarray(L0_ffn_edge_index)[1]),
    }
    nc = bacc.Bacc("TRN2", target_bir_lowering=False, num_devices=1)
    args = {name: nc.dram_tensor(name, a.shape, mybir.dt.from_np(a.dtype), kind="ExternalInput").ap()
            for name, a in arrays.items()}
    args["out"] = nc.dram_tensor("out", [NODES, FEAT], F32, kind="ExternalOutput").ap()
    build(nc, **args)
    result = run_bass_kernel_spmd(nc, [arrays], core_ids=[0])
    return result.results[0]["out"]
```
